# Optimizing a Trainium2 kernel written in Bass

```python
import numpy as np
import jax
import jax.numpy as jnp

def _softmax(x, axis=-1):
    return jax.nn.softmax(x, axis=axis)

def _gelu(x):
    return jax.nn.gelu(x, approximate=True)

def _silu(x):
    return jax.nn.silu(x)

def _sigmoid(x):
    return jax.nn.sigmoid(x)

def _layernorm(x, axis=-1, eps=1e-05):
    m = jnp.mean(x, axis=axis, keepdims=True)
    v = jnp.var(x, axis=axis, keepdims=True)
    return (x - m) / jnp.sqrt(v + eps)

def _scatter_add(tgt, idx, src, axis=0):
    return tgt.at[idx].add(src)

def _segment_sum(src, seg, n):
    return jax.ops.segment_sum(src, seg, n)
kernel_name = 'mk_seq_preln_d2_jaxref_r4_e1b466'

def setup_inputs(seed: int=0):
    np.random.seed(seed)
    _w = jnp.asarray

    def _L0_attn_setup():
        import jax, jax.numpy as jnp
        import numpy as np
        B_, L_, D_, N_, R_ = (2, 512, 512, 16, 64)
        DT_MIN, DT_MAX = (0.001, 0.1)
        key = jax.random.key(seed)
        k0, k1, k2, k3 = jax.random.split(key, 4)
        x = jax.random.normal(k0, (B_, L_, D_), jnp.float32)
        W_xproj = jax.random.normal(k1, (R_ + 2 * N_, D_), jnp.float32) * D_ ** (-0.5)
        dt_std = R_ ** (-0.5)
        W_dt = jax.random.uniform(k2, (D_, R_), jnp.float32, -dt_std, dt_std)
        dt = jnp.exp(jax.random.uniform(k3, (D_,), jnp.float32) * (np.log(DT_MAX) - np.log(DT_MIN)) + np.log(DT_MIN))
        b_dt = dt + jnp.log(-jnp.expm1(-dt))
        A_log = jnp.log(jnp.broadcast_to(jnp.arange(1, N_ + 1, dtype=jnp.float32), (D_, N_)))
        D_param = jnp.ones((D_,), jnp.float32)
        return dict(x=x, W_xproj=W_xproj, W_dt=W_dt, b_dt=b_dt, A_log=A_log, D_param=D_param)
    _L0_attn_in = _L0_attn_setup()

    def _L0_ffn_setup():
        import jax, jax.numpy as jnp
        import numpy as np
        HIDDEN = 512
        INTER = 2048
        SCALE = 64.0

        def fwht(x):
            orig_shape = x.shape
            n = orig_shape[-1]
            x = x.reshape(-1, n)
            h = 1
            while h < n:
                x = x.reshape(-1, n // (2 * h), 2, h)
                a, b = (x[:, :, 0, :], x[:, :, 1, :])
                x = jnp.stack([a + b, a - b], axis=2).reshape(-1, n)
                h *= 2
            return (x / jnp.sqrt(jnp.asarray(n, x.dtype))).reshape(orig_shape)
        key = jax.random.key(seed)
        ks = jax.random.split(key, 8)
        inp = jax.random.normal(ks[0], (4, 512, HIDDEN), dtype=jnp.float32)
        SU_ug = jnp.where(jax.random.bernoulli(ks[1], 0.5, (HIDDEN,)), 1.0, -1.0).astype(jnp.float32)
        SU_dp = jnp.where(jax.random.bernoulli(ks[2], 0.5, (INTER,)), 1.0, -1.0).astype(jnp.float32)
        Wscale_ug = jax.random.uniform(ks[3], (2 * INTER,), jnp.float32, 0.5, 1.5)
        Wscale_dp = jax.random.uniform(ks[4], (HIDDEN,), jnp.float32, 0.5, 1.5)
        W_up = jax.random.normal(ks[5], (INTER, HIDDEN), dtype=jnp.float32) * 0.02
        W_gate = jax.random.normal(ks[6], (INTER, HIDDEN), dtype=jnp.float32) * 0.02
        W_down = jax.random.normal(ks[7], (HIDDEN, INTER), dtype=jnp.float32) * 0.02
        return {'input': inp, 'SU_ug': SU_ug, 'SU_dp': SU_dp, 'Wscale_ug': Wscale_ug, 'Wscale_dp': Wscale_dp, 'W_up': W_up, 'W_gate': W_gate, 'W_down': W_down}
    _L0_ffn_in = _L0_ffn_setup()

    def _L1_attn_setup():
        import jax, jax.numpy as jnp
        import numpy as np
        HIDDEN = 512
        INTER = 1024
        KCONV = 1024
        DT_RANK = 128
        SSM_N = 16
        B_SZ, SEQ = (2, 1024)
        key = jax.random.key(seed)
        ks = jax.random.split(key, 8)
        s = 0.02
        return {'hidden_states': jax.random.normal(ks[0], (B_SZ, SEQ, HIDDEN), jnp.float32), 'W_in': jax.random.normal(ks[1], (2 * INTER, HIDDEN), jnp.float32) * s, 'conv_w': jax.random.normal(ks[2], (INTER, KCONV), jnp.float32) * s, 'W_x': jax.random.normal(ks[3], (DT_RANK + 2 * SSM_N, INTER), jnp.float32) * s, 'W_dt': jax.random.normal(ks[4], (INTER, DT_RANK), jnp.float32) * s, 'b_dt': jax.random.normal(ks[5], (INTER,), jnp.float32) * s, 'D': jnp.ones((INTER,), jnp.float32), 'W_out': jax.random.normal(ks[6], (HIDDEN, INTER), jnp.float32) * s}
    _L1_attn_in = _L1_attn_setup()

    def _L1_ffn_setup():
        import jax, jax.numpy as jnp
        import numpy as np
        E = 64
        K = 8
        H = 512
        I = 192
        CAP = 128

        def _moe(hidden_states, gate_w, wg, wu, wd):
            B, S, Hd = hidden_states.shape
            x = hidden_states.reshape(-1, Hd)
            T = x.shape[0]
            logits = x @ gate_w.T
            probs = jax.nn.softmax(logits.astype(jnp.float32), axis=-1)
            w, sel = jax.lax.top_k(probs, K)
            w = w / jnp.sum(w, axis=-1, keepdims=True)
            w = w.astype(x.dtype)
            eid = sel.reshape(-1)
            tok = jnp.repeat(jnp.arange(T), K)
            oh = jax.nn.one_hot(eid, E, dtype=jnp.int32)
            pos = jnp.sum(jnp.cumsum(oh, axis=0) * oh, axis=-1) - 1
            valid = pos < CAP
            slot = jnp.where(valid, pos, CAP)
            xin = jnp.zeros((E, CAP + 1, Hd), x.dtype).at[eid, slot].set(x[tok])
            inp = xin[:, :CAP]
            h = jax.nn.silu(jnp.einsum('ech,ehi->eci', inp, wg)) * jnp.einsum('ech,ehi->eci', inp, wu)
            out = jnp.einsum('eci,eih->ech', h, wd)
            out_pad = jnp.concatenate([out, jnp.zeros((E, 1, Hd), out.dtype)], axis=1)
            g = out_pad[eid, slot] * (w.reshape(-1) * valid.astype(w.dtype))[:, None]
            y = jnp.zeros((T, Hd), x.dtype).at[tok].add(g)
            return y.reshape(B, S, Hd)
        key = jax.random.key(seed)
        k1, k2, k3, k4, k5 = jax.random.split(key, 5)
        hidden_states = jax.random.normal(k1, (1, 512, H), dtype=jnp.float32)
        gate_w = jax.random.normal(k2, (E, H), dtype=jnp.float32) * 0.02
        wg = jax.random.normal(k3, (E, H, I), dtype=jnp.float32) * 0.02
        wu = jax.random.normal(k4, (E, H, I), dtype=jnp.float32) * 0.02
        wd = jax.random.normal(k5, (E, I, H), dtype=jnp.float32) * 0.02
        return {'hidden_states': hidden_states, 'gate_w': gate_w, 'wg': wg, 'wu': wu, 'wd': wd}
    _L1_ffn_in = _L1_ffn_setup()
    _d = {'L0_attn_x': _L0_attn_in['x'], 'L0_attn_W_xproj': _L0_attn_in['W_xproj'], 'L0_attn_W_dt': _L0_attn_in['W_dt'], 'L0_attn_b_dt': _L0_attn_in['b_dt'], 'L0_attn_A_log': _L0_attn_in['A_log'], 'L0_attn_D_param': _L0_attn_in['D_param'], 'L0_ffn_SU_ug': _L0_ffn_in['SU_ug'], 'L0_ffn_SU_dp': _L0_ffn_in['SU_dp'], 'L0_ffn_Wscale_ug': _L0_ffn_in['Wscale_ug'], 'L0_ffn_Wscale_dp': _L0_ffn_in['Wscale_dp'], 'L0_ffn_W_up': _L0_ffn_in['W_up'], 'L0_ffn_W_gate': _L0_ffn_in['W_gate'], 'L0_ffn_W_down': _L0_ffn_in['W_down'], 'L1_attn_W_in': _L1_attn_in['W_in'], 'L1_attn_conv_w': _L1_attn_in['conv_w'], 'L1_attn_W_x': _L1_attn_in['W_x'], 'L1_attn_W_dt': _L1_attn_in['W_dt'], 'L1_attn_b_dt': _L1_attn_in['b_dt'], 'L1_attn_D': _L1_attn_in['D'], 'L1_attn_W_out': _L1_attn_in['W_out'], 'L1_ffn_gate_w': _L1_ffn_in['gate_w'], 'L1_ffn_wg': _L1_ffn_in['wg'], 'L1_ffn_wu': _L1_ffn_in['wu'], 'L1_ffn_wd': _L1_ffn_in['wd']}
    _x0 = _d['L0_attn_x']
    _d['L0_attn_x'] = jax.random.normal(jax.random.fold_in(jax.random.key(seed), 1), (1, 2048, 512), dtype=_x0.dtype)
    del _x0
    return _d

def reference(L0_attn_x, L0_attn_W_xproj, L0_attn_W_dt, L0_attn_b_dt, L0_attn_A_log, L0_attn_D_param, L0_ffn_SU_ug, L0_ffn_SU_dp, L0_ffn_Wscale_ug, L0_ffn_Wscale_dp, L0_ffn_W_up, L0_ffn_W_gate, L0_ffn_W_down, L1_attn_W_in, L1_attn_conv_w, L1_attn_W_x, L1_attn_W_dt, L1_attn_b_dt, L1_attn_D, L1_attn_W_out, L1_ffn_gate_w, L1_ffn_wg, L1_ffn_wu, L1_ffn_wd):

    def _L0_attn_ref(x, W_xproj, W_dt, b_dt, A_log, D_param):
        import jax, jax.numpy as jnp
        import numpy as np
        B_, L_, D_, N_, R_ = (2, 512, 512, 16, 64)
        DT_MIN, DT_MAX = (0.001, 0.1)
        R = W_dt.shape[1]
        N = A_log.shape[1]
        x_dbl = jnp.einsum('bld,ed->ble', x, W_xproj)
        delta_raw, Bm, Cm = jnp.split(x_dbl, [R, R + N], axis=-1)
        delta = jax.nn.softplus(jnp.einsum('blr,dr->bld', delta_raw, W_dt) + b_dt)
        A = -jnp.exp(A_log)
        dA = jnp.exp(jnp.einsum('bld,dn->bldn', delta, A))
        dBx = jnp.einsum('bld,bln->bldn', delta * x, Bm)

        def step(h, inp):
            dA_t, dBx_t, C_t = inp
            h = dA_t * h + dBx_t
            y_t = jnp.einsum('bdn,bn->bd', h, C_t)
            return (h, y_t)
        h0 = jnp.zeros((x.shape[0], x.shape[2], N), x.dtype)
        xs = (jnp.moveaxis(dA, 1, 0), jnp.moveaxis(dBx, 1, 0), jnp.moveaxis(Cm, 1, 0))
        _, ys = jax.lax.scan(step, h0, xs)
        y = jnp.moveaxis(ys, 0, 1)
        return y + x * D_param

    def _L0_ffn_ref(input, SU_ug, SU_dp, Wscale_ug, Wscale_dp, W_up, W_gate, W_down):
        import jax, jax.numpy as jnp
        import numpy as np
        HIDDEN = 512
        INTER = 2048
        SCALE = 64.0

        def fwht(x):
            orig_shape = x.shape
            n = orig_shape[-1]
            x = x.reshape(-1, n)
            h = 1
            while h < n:
                x = x.reshape(-1, n // (2 * h), 2, h)
                a, b = (x[:, :, 0, :], x[:, :, 1, :])
                x = jnp.stack([a + b, a - b], axis=2).reshape(-1, n)
                h *= 2
            return (x / jnp.sqrt(jnp.asarray(n, x.dtype))).reshape(orig_shape)
        n = SU_ug.shape[0]
        x = input.reshape(-1, n)
        x = fwht(x * SU_ug) / SCALE
        x_up = x @ W_up.T * (Wscale_ug[:INTER] * SCALE)
        x_gate = x @ W_gate.T * (Wscale_ug[INTER:] * SCALE)
        x = jax.nn.silu(x_gate) * x_up
        x = fwht(x * SU_dp) / SCALE
        x = x @ W_down.T * (Wscale_dp * SCALE)
        return x.reshape(input.shape)

    def _L1_attn_ref(hidden_states, W_in, conv_w, W_x, W_dt, b_dt, D, W_out):
        import jax, jax.numpy as jnp
        import numpy as np
        HIDDEN = 512
        INTER = 1024
        KCONV = 1024
        DT_RANK = 128
        SSM_N = 16
        B_SZ, SEQ = (2, 1024)
        xz = jnp.einsum('bsh,ih->bsi', hidden_states, W_in)
        x, z = jnp.split(xz, 2, axis=-1)
        x = jnp.einsum('bsk,ik->bsi', x, conv_w)
        x_proj = jnp.einsum('bsi,pi->bsp', x, W_x)
        delta_raw = x_proj[..., :DT_RANK]
        B = x_proj[..., DT_RANK:DT_RANK + SSM_N]
        C = x_proj[..., DT_RANK + SSM_N:]
        delta = jax.nn.softplus(jnp.einsum('bsr,ir->bsi', delta_raw, W_dt))
        y = x * D
        z = jax.nn.silu(z)
        return jnp.einsum('bsi,hi->bsh', y * z, W_out)

    def _L1_ffn_ref(hidden_states, gate_w, wg, wu, wd):
        import jax, jax.numpy as jnp
        import numpy as np
        E = 64
        K = 8
        H = 512
        I = 192
        CAP = 128

        def _moe(hidden_states, gate_w, wg, wu, wd):
            B, S, Hd = hidden_states.shape
            x = hidden_states.reshape(-1, Hd)
            T = x.shape[0]
            logits = x @ gate_w.T
            probs = jax.nn.softmax(logits.astype(jnp.float32), axis=-1)
            w, sel = jax.lax.top_k(probs, K)
            w = w / jnp.sum(w, axis=-1, keepdims=True)
            w = w.astype(x.dtype)
            eid = sel.reshape(-1)
            tok = jnp.repeat(jnp.arange(T), K)
            oh = jax.nn.one_hot(eid, E, dtype=jnp.int32)
            pos = jnp.sum(jnp.cumsum(oh, axis=0) * oh, axis=-1) - 1
            valid = pos < CAP
            slot = jnp.where(valid, pos, CAP)
            xin = jnp.zeros((E, CAP + 1, Hd), x.dtype).at[eid, slot].set(x[tok])
            inp = xin[:, :CAP]
            h = jax.nn.silu(jnp.einsum('ech,ehi->eci', inp, wg)) * jnp.einsum('ech,ehi->eci', inp, wu)
            out = jnp.einsum('eci,eih->ech', h, wd)
            out_pad = jnp.concatenate([out, jnp.zeros((E, 1, Hd), out.dtype)], axis=1)
            g = out_pad[eid, slot] * (w.reshape(-1) * valid.astype(w.dtype))[:, None]
            y = jnp.zeros((T, Hd), x.dtype).at[tok].add(g)
            return y.reshape(B, S, Hd)
        return _moe(hidden_states, gate_w, wg, wu, wd)
    x = L0_attn_x
    x = x + _L0_attn_ref(_layernorm(x, axis=-1), L0_attn_W_xproj, L0_attn_W_dt, L0_attn_b_dt, L0_attn_A_log, L0_attn_D_param)
    x = x + _L0_ffn_ref(_layernorm(x, axis=-1), L0_ffn_SU_ug, L0_ffn_SU_dp, L0_ffn_Wscale_ug, L0_ffn_Wscale_dp, L0_ffn_W_up, L0_ffn_W_gate, L0_ffn_W_down)
    x = x + _L1_attn_ref(_layernorm(x, axis=-1), L1_attn_W_in, L1_attn_conv_w, L1_attn_W_x, L1_attn_W_dt, L1_attn_b_dt, L1_attn_D, L1_attn_W_out)
    x = x + _L1_ffn_ref(_layernorm(x, axis=-1), L1_ffn_gate_w, L1_ffn_wg, L1_ffn_wu, L1_ffn_wd)
    return x

_drawn_inputs = setup_inputs


def setup_inputs(seed=0):
    import zlib

    import numpy as np

    out = dict(_drawn_inputs(seed))
    spreads = {'L0_attn_D_param': (1.0, 0.2), 'L1_attn_D': (1.0, 0.6)}
    factors = {'L0_ffn_Wscale_dp': 3.878,
     'L1_ffn_gate_w': 8.0,
     'L1_ffn_wg': 8.0,
     'L1_ffn_wu': 8.0,
     'L1_ffn_wd': 8.0}
    for name, (base, spread) in spreads.items():
        noise = np.random.default_rng([zlib.crc32(name.encode()), seed]).standard_normal(out[name].shape)
        drawn = base * np.exp(spread * noise) if base else spread * noise
        out[name] = jnp.asarray(drawn.astype(out[name].dtype))
    for name, factor in factors.items():
        out[name] = (out[name] * factor).astype(out[name].dtype)
    return out
```

```python
import numpy as np

T, D = 2048, 512
P = 128
CH = 512
NCH = T // CH
TT = CH // P
KT = D // P
NS = 16
R = 64
F0 = 2048
M0 = F0 // P
HALF = M0 // 2
I1 = 1024
M1 = I1 // P
E, TOPK, CAP, FE = 64, 8, 128, 192
FH = FE // 2
ROW = D + E + 1
NROWS = T + P
FAR = 1.0e6
EPS = 1e-5
SLOTS = 4


def hadamard(n):
    i = np.arange(n)
    v = i[:, None] & i[None, :]
    odd = np.zeros((n, n), np.int64)
    for b in range(n.bit_length()):
        odd += (v >> b) & 1
    return np.where(odd % 2, -1.0, 1.0)


H4 = hadamard(4).astype(int)


def build(nc, a):
    import concourse.bass as bass
    from concourse import mybir
    from contextlib import ExitStack

    fp32, f32r, bf16, u32 = mybir.dt.float32, mybir.dt.float32r, mybir.dt.bfloat16, mybir.dt.uint32
    ALU, ACT, AX = mybir.AluOpType, mybir.ActivationFunctionType, mybir.AxisListType
    ds = bass.ds
    top = ExitStack()
    sem = lambda n: top.enter_context(nc.semaphore(n))

    def wait(eng, s, v):
        if not (isinstance(v, int) and v <= 0):
            eng.wait_ge(s, v)

    def sb(ctx, name, shape, dt=fp32):
        return ctx.enter_context(nc.sbuf_tensor(name, shape, dt))

    def chunk(tensor, c):
        return tensor[ds(c * CH, CH), :].rearrange("(t p) d -> p t d", p=P)

    acc = [a["acc0"], a["acc1"]]

    class Norm:

        def __init__(self, n):
            self.bn = sem(n + "_bn")
            self.mv = sem(n + "_mv")
            self.ve = sem(n + "_ve")
            self.rs = sem(n + "_rs")
            self.xn = sem(n + "_xn")
            self.tp = sem(n + "_tp")
            self.xT = sem(n + "_xT")
            self.lo = sem(n + "_lo")

    with top:
        S_const = sem("constants_ready")
        small = top.enter_context(ExitStack())
        ident = sb(small, "ident", [P, P])
        st6 = sb(small, "st6", [P, TT, 6])
        mv = sb(small, "mv", [P, TT, 2])
        ve = sb(small, "ve", [P, TT])
        rs = sb(small, "rs", [P, TT])
        neghalf = sb(small, "neghalf", [P, TT])
        eps = sb(small, "eps", [P, TT])
        bank = [top.enter_context(nc.psum_tensor(f"bank{i}", [P, 512], fp32)) for i in range(8)]

        def norm_stats(dve, n, c, src):
            for t in range(TT):
                last = nc.vector.bn_stats(st6[:, t, :], src[:, t, :])
            last.then_inc(n.bn, 1)
            dve.wait_ge(S_const, 1)
            dve.wait_ge(n.bn, c + 1)
            for t in range(TT):
                last = nc.vector.bn_aggr(mv[:, t, :], st6[:, t, :])
            last.then_inc(n.mv, 1)

        def norm_rstd(pool, n, c):
            pool.wait_ge(S_const, 1)
            pool.wait_ge(n.mv, c + 1)
            nc.gpsimd.tensor_tensor(ve[:, :], mv[:, :, 1], eps[:, :], ALU.add).then_inc(n.ve, 1)
            pool.wait_ge(n.ve, c + 1)
            nc.gpsimd.tensor_tensor(rs[:, :], ve[:, :], neghalf[:, :], ALU.pow).then_inc(n.rs, 1)

        def normalize(n, t, dst, src):
            return nc.vector.tensor_scalar(dst, src[:, t, :], mv[:, t, 0:1], rs[:, t:t + 1],
                                           ALU.subtract, ALU.mult).then_inc(n.xn, 1)

        A = ExitStack()
        with A:
            wug = sb(A, "wug", [P, KT, 2 * F0])
            wdn = sb(A, "wdn", [P, M0, D])
            had = sb(A, "had", [P, 2, P])
            wxp = sb(A, "wxp", [P, KT, P])
            wdt = sb(A, "wdt", [R, D])
            sel = sb(A, "sel", [P, 2 * NS], f32r)
            self32 = sb(A, "self32", [P, 2 * NS])
            vec = sb(A, "vec", [P, 3 * KT + 3 * M0])
            b_dt, dpar, su_ug = vec[:, 0:KT], vec[:, KT:2 * KT], vec[:, 2 * KT:3 * KT]
            o = 3 * KT
            su_dp, wsg, wsu = (vec[:, o + i * M0:o + (i + 1) * M0] for i in range(3))
            an = sb(A, "an", [P, KT, NS])
            gsh = sb(A, "gsh", [P, M0])
            cs = sb(A, "cs", [P, M0])
            state = sb(A, "state", [P, KT, NS])
            xin = sb(A, "xin", [P, TT, D])
            xnt = sb(A, "xnt", [P, 2, D])
            y = sb(A, "y", [P, KT, CH])
            dl = sb(A, "dl", [P, KT, CH])
            u = sb(A, "u", [P, KT, CH])
            dA = [sb(A, f"dA{i}", [P, KT, CH]) for i in range(2)]
            bx = [sb(A, f"bx{i}", [P, KT, CH]) for i in range(2)]
            dtr = xnt[0:R, 0, :]
            xdr = sb(A, "xdr", [P, CH], f32r)
            x1 = sb(A, "x1", [P, TT, D])
            wsdp = x1[:, TT - 1, :]
            xn2T = sb(A, "xn2T", [P, KT, CH])
            act8 = sb(A, "act8", [P, HALF, CH])
            th = sb(A, "th", [P, 2, CH])
            raw = [act8[:, 4 * i:4 * i + 4, :] for i in range(2)]
            PB, PC, PF = bank[0:2], bank[2:4], bank[4:8]
            HB = [bank[0], bank[1], bank[2], bank[3]]

            n1, n2 = Norm("n1"), Norm("n2")
            S_x = sem("x_in"); S_w = sem("weights_in")
            S_raw = [sem("raw_in0"), sem("raw_in1")]
            S_wsc = sem("raw_scaled"); S_pmm = sem("prep_mm"); S_pev = sem("prep_ev")
            S_bf = sem("butterfly"); S_bc = sem("butterfly_copied"); S_sel = sem("selectors")
            S_an = sem("decay_rates"); S_cs = sem("scales_ready"); S_st0 = sem("state_zeroed")
            S_xd = sem("xdbl_mm"); S_hi = sem("xdbl_hi"); S_h2 = sem("xdbl_split"); S_dt = sem("dt_mm")
            S_abs = sem("sp_abs"); S_exp = sem("sp_exp"); S_ln = sem("sp_ln"); S_rel = sem("sp_relu")
            S_sp = sem("sp_sum"); S_dl = sem("delta_ready"); S_u = sem("u_ready"); S_yi = sem("y_init")
            S_bb = sem("b_bcast"); S_cb = sem("c_bcast"); S_dA = sem("dA_ready"); S_bm = sem("bx_made")
            S_sc = sem("scanned"); S_sv = sem("state_saved"); S_cm = sem("h_weighted"); S_ya = sem("y_added")
            S_yT = sem("y_transposed"); S_x1 = sem("x1_made")
            S_g = sem("gate_mm"); S_up = sem("up_mm"); S_th = sem("tanh_done"); S_hg = sem("half_gated")
            S_gt = sem("gated"); S_dm = sem("down_mm"); S_de = sem("down_added"); S_x2 = sem("x2_stored")
            S_fill = sem("slots_filled"); S_z = sem("fill_tile")
            fill = th[:, :, :].rearrange("p a b -> p (a b)")[:, 0:ROW]

            ffn_steps = [("up", j) for j in range(HALF)] + [("down", 0)] + \
                        [("up", j) for j in range(HALF, M0)] + [("down", 1)]
            ffn_slots = [[s] for s in ffn_steps[:4]] + [[s] for s in ffn_steps[4:]] + [[], []]
            GROUPS = 12

            with nc.Block() as block:
                @block.sync
                def _(sp):
                    def load_x(c):
                        wait(sp, S_x1, 4 * c)
                        sp.dma_start(xin[:, :, :], chunk(a["x"][0], c)).then_inc(S_x, 16)

                    def raw_group(g):
                        if g >= 2:
                            sp.wait_ge(S_pmm, 4 * (g - 1))
                        if g < 4:
                            src = a["wdT"].rearrange("(m p) h -> p m h", p=P)[:, 4 * g:4 * g + 4, :]
                        else:
                            w = a["wgT"] if g < 8 else a["wuT"]
                            b = g % 4
                            src = w.rearrange("(k p) i -> p k i", p=P)[:, :, 512 * b:512 * b + 512]
                        sp.dma_start(raw[g % 2], src).then_inc(S_raw[g % 2], 16)

                    load_x(0)
                    for dst, src in ((ident[:, :], a["ident"]), (wxp[:, :, 0:96], a["wxpT"].rearrange("(k p) e -> p k e", p=P)),
                                     (wxp[:, :, 96:P], a["wxpT"][:, 64:96].rearrange("(k p) e -> p k e", p=P)),
                                     (wdt[:, :], a["wdtT"]), (vec[:, :], a["vec"]),
                                     (an[:, :, :], a["A_log"].rearrange("(k p) n -> p k n", p=P)),
                                     (had[:, :, :], a["had"].rearrange("p (s q) -> p s q", s=2)),
                                     (self32[:, :], a["sel"]),
                                     (wsdp, a["ws_dp"].unsqueeze(0).to_broadcast([P, D]))):
                        sp.dma_start(dst, src).then_inc(S_w, 16)
                    for g in range(GROUPS):
                        raw_group(g)
                    sp.wait_ge(S_z, 2)
                    sp.dma_start(a["slots"].rearrange("(e p) c -> p e c", p=P),
                                 fill.unsqueeze(1).to_broadcast([P, E, ROW])).then_inc(S_fill, 16)
                    for v in acc:
                        sp.dma_start(v[T:NROWS, :], fill[:, 0:D]).then_inc(S_fill, 16)
                    sp.dma_start(acc[1][0:T, :].rearrange("(t p) d -> p t d", p=P),
                                 fill[:, 0:D].unsqueeze(1).to_broadcast([P, NCH * TT, D])).then_inc(S_fill, 16)
                    load_x(1)
                    with sp.Fori(1, NCH - 1) as c:
                        sp.wait_ge(S_de, 8 * c)
                        sp.dma_start(chunk(a["x2"], c - 1), x1[:, :, :]).then_inc(S_x2, 16)
                        sp.wait_ge(S_x1, 4 * c + 4)
                        sp.dma_start(xin[:, :, :], chunk(a["x"][0], c + 1)).then_inc(S_x, 16)
                    for c in (NCH - 2, NCH - 1):
                        sp.wait_ge(S_de, 8 * (c + 1))
                        sp.dma_start(chunk(a["x2"], c), x1[:, :, :]).then_inc(S_x2, 16)
                    sp.wait_ge(S_x2, 16 * NCH)
                    sp.wait_ge(S_fill, 64)

                @block.tensor
                def _(pe):
                    def transposes(n, c, t, b):
                        pe.wait_ge(n.xn, 4 * c + t + 1)
                        for k in range(KT):
                            last = nc.tensor.transpose(b[:, k * P:(k + 1) * P], xnt[:, t % 2, k * P:(k + 1) * P], ident[:, :])
                        last.then_inc(n.tp, 1)

                    def head(c, ffn):
                        wait(pe, S_bm, NS * c)
                        wait(pe, S_cm, NS * c)
                        wait(pe, n2.xT, 4 * c)
                        for t in range(TT):
                            transposes(n1, c, t, HB[t])
                        ffn(0)
                        pe.wait_ge(n1.xT, 4 * c + 4)
                        for k in range(KT):
                            last = nc.tensor.matmul(HB[0][:, :], wxp[:, k, :], y[:, k, :], start=(k == 0), stop=(k == KT - 1))
                        last.then_inc(S_xd, 1)
                        ffn(1)
                        pe.wait_ge(S_h2, c + 1)
                        for k in range(KT):
                            nc.tensor.matmul(HB[(k + 1) % 4][:, :], wdt[:, k * P:(k + 1) * P], dtr,
                                             start=True, stop=True).then_inc(S_dt, 1)
                        ffn(2)
                        ffn(3)
                        pe.wait_ge(S_rel, 4 * c + 4)

                    def bcast(c, n):
                        wait(pe, S_bm, NS * c + n - 1 if n >= 2 else 0)
                        nc.tensor.matmul(PB[n % 2][:, :], sel[:, n:n + 1].to_broadcast([P, P]), xdr[:, :],
                                         start=True, stop=True).then_inc(S_bb, 1)
                        wait(pe, S_cm, NS * c + n - 1 if n >= 2 else 0)
                        nc.tensor.matmul(PC[n % 2][:, :], sel[:, NS + n:NS + n + 1].to_broadcast([P, P]), xdr[:, :],
                                         start=True, stop=True).then_inc(S_cb, 1)

                    def tail(c):
                        wait(pe, S_de, 8 * c)
                        pe.wait_ge(S_ya, NS * (c + 1))
                        for t in range(TT):
                            for k in range(KT):
                                last = nc.tensor.transpose(PF[t][:, k * P:(k + 1) * P], y[:, k, t * P:(t + 1) * P], ident[:, :])
                            last.then_inc(S_yT, 1)
                        for t in range(TT):
                            transposes(n2, c, t, HB[t])

                    def ffn_step(c, kind, j):
                        if kind == "up":
                            if j == 0:
                                pe.wait_ge(n2.xT, 4 * c + 4)
                            if j == HALF:
                                pe.wait_ge(S_de, 8 * c + 4)
                            if j % HALF >= 2:
                                pe.wait_ge(S_gt, M0 * c + j - 1)
                            for which, s in ((0, S_g), (1, S_up)):
                                b = PF[2 * (j % 2) + which]
                                for k in range(KT):
                                    w0 = which * F0 + j * P
                                    last = nc.tensor.matmul(b[:, :], wug[:, k, w0:w0 + P], xn2T[:, k, :],
                                                            start=(k == 0), stop=(k == KT - 1))
                                last.then_inc(s, 1)
                        else:
                            pe.wait_ge(S_gt, M0 * c + HALF * (j + 1))
                            for t in range(TT):
                                for k in range(HALF):
                                    last = nc.tensor.matmul(PF[t][:, :], act8[:, k, t * P:(t + 1) * P], wdn[:, HALF * j + k, :],
                                                            start=(k == 0), stop=(k == HALF - 1))
                                last.then_inc(S_dm, 1)

                    def ffn(c):
                        return lambda slot: [ffn_step(c, *s) for s in ffn_slots[slot]]

                    def prep(g):
                        pe.wait_ge(S_raw[g % 2], 16 * (g // 2 + 1))
                        if g < 4:
                            pe.wait_ge(S_wsc, g + 1)
                        for m in range(4):
                            wait(pe, S_pev, 4 * (g - 1) + m + 1 if g else 0)
                            for k in range(4):
                                last = nc.tensor.matmul(PF[m][:, :], had[:, 0 if H4[m][k] > 0 else 1, :], raw[g % 2][:, k, :],
                                                        start=(k == 0), stop=(k == 3))
                            last.then_inc(S_pmm, 1)

                    pe.wait_ge(S_w, 16 * 9)
                    pe.wait_ge(S_sel, 1)
                    head(0, lambda slot: None)
                    for n in range(NS):
                        bcast(0, n)
                        if n < GROUPS:
                            prep(n)
                    pe.wait_ge(S_pev, 4 * GROUPS)
                    pe.wait_ge(S_bf, 8)
                    pe.wait_ge(S_bc, 4)
                    tail(0)
                    with pe.Fori(1, NCH) as c:
                        f = ffn(c - 1)
                        head(c, f)
                        for n in range(NS):
                            bcast(c, n)
                            f(4 + n)
                        tail(c)
                    for slot in range(len(ffn_slots)):
                        ffn(NCH - 1)(slot)

                @block.scalar
                def _(act):
                    def evac(n, c, t, b, dst):
                        act.wait_ge(n.tp, 4 * c + t + 1)
                        nc.scalar.activation(dst[:, :, t * P:(t + 1) * P], b[:, :].rearrange("p (k q) -> p k q", k=KT),
                                             ACT.Copy).then_inc(n.xT, 1)

                    def head(c, ffn):
                        for t in range(TT):
                            evac(n1, c, t, HB[t], y)
                        ffn(0)
                        act.wait_ge(S_xd, c + 1)
                        nc.scalar.activation(dtr, HB[0][0:R, :], ACT.Copy)
                        nc.scalar.activation(xdr[:, :], HB[0][:, :], ACT.Copy).then_inc(S_hi, 1)
                        ffn(1)
                        for k in range(KT):
                            act.wait_ge(S_dt, 4 * c + k + 1)
                            nc.scalar.activation(dl[:, k, :], HB[(k + 1) % 4][:, :], ACT.Abs, bias=b_dt[:, k:k + 1]).then_inc(S_abs, 1)
                        act.wait_ge(S_abs, 4 * c + 4)
                        nc.scalar.activation(dl[:, :, :], dl[:, :, :], ACT.Exp, scale=-1.0).then_inc(S_exp, 1)
                        ffn(2)
                        act.wait_ge(S_exp, c + 1)
                        nc.scalar.activation(u[:, :, :], dl[:, :, :], ACT.Ln, bias=1.0).then_inc(S_ln, 1)
                        ffn(3)
                        act.wait_ge(S_u, c + 1)
                        for k in range(KT):
                            last = nc.scalar.activation(y[:, k, :], y[:, k, :], ACT.Copy, scale=dpar[:, k:k + 1])
                        last.then_inc(S_yi, 1)

                    def decay(c, n):
                        wait(act, S_sc, NS * c + n - 1)
                        for k in range(KT):
                            last = nc.scalar.activation(dA[n % 2][:, k, :], dl[:, k, :], ACT.Exp, scale=an[:, k, n:n + 1])
                        last.then_inc(S_dA, 1)

                    def tail(c):
                        for t in range(TT):
                            evac(n2, c, t, HB[t], xn2T)

                    def ffn_step(c, kind, j):
                        if kind == "up":
                            act.wait_ge(S_g, M0 * c + j + 1)
                            if j >= 2:
                                act.wait_ge(S_gt, M0 * c + j - 1)
                            nc.scalar.activation(th[:, j % 2, :], PF[2 * (j % 2)][:, :], ACT.Tanh, scale=gsh[:, j:j + 1]).then_inc(S_th, 1)

                    def ffn(c):
                        return lambda slot: [ffn_step(c, *s) for s in ffn_slots[slot]]

                    def prep(g):
                        for m in range(4):
                            act.wait_ge(S_pmm, 4 * g + m + 1)
                            if g < 4:
                                nc.scalar.activation(wdn[:, 4 * g + m, :], PF[m][:, :], ACT.Copy).then_inc(S_pev, 1)
                            else:
                                b = g - 4
                                nc.scalar.activation(wug[:, m, 512 * b:512 * b + 512], PF[m][:, :], ACT.Copy,
                                                     scale=su_ug[:, m:m + 1]).then_inc(S_pev, 1)

                    def butterfly_copy(i):
                        lo = (0, 2, 0, 1)[i]
                        act.wait_ge(S_bf, 2 * i + 2)
                        nc.scalar.activation(wdn[:, 4 * lo:4 * lo + 4, :], (x1, xn2T)[i % 2][:, :, :], ACT.Copy).then_inc(S_bc, 1)

                    act.wait_ge(S_w, 16 * 9)
                    nc.scalar.activation(an[:, :, :], an[:, :, :], ACT.Exp).then_inc(S_an, 1)
                    nc.scalar.activation(sel[:, :], self32[:, :], ACT.Copy).then_inc(S_sel, 1)
                    head(0, lambda slot: None)
                    act.wait_ge(S_an, 2)
                    for n in range(NS):
                        if n == 0:
                            act.wait_ge(S_dl, 1)
                        decay(0, n)
                        if n < GROUPS:
                            prep(n)
                        if n >= 10 and n % 2 == 0:
                            butterfly_copy((n - 10) // 2)
                    butterfly_copy(3)
                    act.wait_ge(S_cs, 4)
                    act.wait_ge(S_fill, 64)
                    tail(0)
                    with act.Fori(1, NCH) as c:
                        f = ffn(c - 1)
                        head(c, f)
                        act.wait_ge(S_dl, c + 1)
                        for n in range(NS):
                            decay(c, n)
                            f(4 + n)
                        tail(c)
                    for slot in range(len(ffn_slots)):
                        ffn(NCH - 1)(slot)

                @block.vector
                def _(dve):
                    def norm(n, c, src):
                        norm_stats(dve, n, c, src)
                        dve.wait_ge(n.rs, c + 1)
                        for t in range(TT):
                            if t >= 2:
                                dve.wait_ge(n.tp, 4 * c + t - 1)
                            normalize(n, t, xnt[:, t % 2, :], src)

                    def head(c, ffn):
                        dve.wait_ge(S_x, 16 * (c + 1))
                        wait(dve, n2.tp, 4 * c)
                        norm(n1, c, xin)
                        ffn(0)
                        dve.wait_ge(S_hi, c + 1)
                        nc.vector.tensor_tensor(xdr[96:P, :], HB[0][96:P, :], xdr[96:P, :].bitcast(fp32), ALU.subtract).then_inc(S_h2, 1)
                        ffn(1)
                        wait(dve, S_ya, NS * c)
                        for k in range(KT):
                            dve.wait_ge(S_abs, 4 * c + k + 1)
                            nc.vector.tensor_scalar(bx[0][:, k, :], HB[(k + 1) % 4][:, :], b_dt[:, k:k + 1], 0.0, ALU.add, ALU.max).then_inc(S_rel, 1)
                        ffn(2)
                        dve.wait_ge(S_exp, c + 1)
                        nc.vector.tensor_scalar(bx[1][:, :, :], dl[:, :, :], 1.0, 1.0, ALU.add, ALU.subtract).then_inc(S_sp, 1)
                        dve.wait_ge(S_sp, 3 * c + 1)
                        nc.vector.tensor_tensor(bx[1][:, :, :], dl[:, :, :], bx[1][:, :, :], ALU.subtract).then_inc(S_sp, 1)
                        dve.wait_ge(S_sp, 3 * c + 2)
                        nc.vector.tensor_tensor(bx[1][:, :, :], bx[1][:, :, :], bx[0][:, :, :], ALU.add).then_inc(S_sp, 1)
                        ffn(3)
                        dve.wait_ge(S_ln, c + 1)
                        dve.wait_ge(S_sp, 3 * c + 3)
                        nc.vector.tensor_tensor(dl[:, :, :], u[:, :, :], bx[1][:, :, :], ALU.add).then_inc(S_dl, 1)
                        dve.wait_ge(S_dl, c + 1)
                        nc.vector.tensor_tensor(u[:, :, :], dl[:, :, :], y[:, :, :], ALU.mult).then_inc(S_u, 1)

                    def scan(c, n, ffn):
                        b, i = bx[n % 2], NS * c + n
                        dve.wait_ge(S_bb, i + 1)
                        wait(dve, S_ya, i - 1)
                        if n == 0:
                            dve.wait_ge(S_u, c + 1)
                        nc.vector.tensor_tensor(b[:, :, :], u[:, :, :], PB[n % 2][:, :].unsqueeze(1).to_broadcast([P, KT, CH]),
                                                ALU.mult).then_inc(S_bm, 1)
                        dve.wait_ge(S_dA, i + 1)
                        dve.wait_ge(S_bm, i + 1)
                        for k in range(KT):
                            last = nc.vector.tensor_tensor_scan(b[:, k, :], dA[n % 2][:, k, :], b[:, k, :], state[:, k, n:n + 1],
                                                                ALU.mult, ALU.add)
                        last.then_inc(S_sc, 1)
                        ffn(4 + n)
                        dve.wait_ge(S_sc, i + 1)
                        nc.vector.tensor_copy(state[:, :, n:n + 1], b[:, :, CH - 1:CH]).then_inc(S_sv, 1)
                        dve.wait_ge(S_cb, i + 1)
                        dve.wait_ge(S_sv, i + 1)
                        nc.vector.tensor_tensor(b[:, :, :], b[:, :, :], PC[n % 2][:, :].unsqueeze(1).to_broadcast([P, KT, CH]),
                                                ALU.mult).then_inc(S_cm, 1)

                    def tail(c):
                        wait(dve, S_x2, 16 * c)
                        for t in range(TT):
                            dve.wait_ge(S_yT, 4 * c + t + 1)
                            nc.vector.tensor_tensor(x1[:, t, :], xin[:, t, :], PF[t][:, :], ALU.add).then_inc(S_x1, 1)
                        dve.wait_ge(S_x1, 4 * c + 4)
                        dve.wait_ge(n1.tp, 4 * c + 4)
                        norm(n2, c, x1)

                    def ffn_step(c, kind, j):
                        if kind == "up":
                            g, up = PF[2 * (j % 2)], PF[2 * (j % 2) + 1]
                            dve.wait_ge(S_th, M0 * c + j + 1)
                            nc.vector.scalar_tensor_tensor(out=th[:, j % 2, :], in0=th[:, j % 2, :], scalar=1.0, in1=g[:, :],
                                                           op0=ALU.add, op1=ALU.mult).then_inc(S_hg, 1)
                            dve.wait_ge(S_up, M0 * c + j + 1)
                            dve.wait_ge(S_hg, M0 * c + j + 1)
                            nc.vector.scalar_tensor_tensor(out=act8[:, j % HALF, :], in0=up[:, :], scalar=cs[:, j:j + 1],
                                                           in1=th[:, j % 2, :], op0=ALU.mult, op1=ALU.mult).then_inc(S_gt, 1)
                        else:
                            for t in range(TT):
                                dve.wait_ge(S_dm, 8 * c + 4 * j + t + 1)
                                if j == 1:
                                    dve.wait_ge(S_de, 8 * c + t + 1)
                                nc.vector.tensor_tensor(x1[:, t, :], x1[:, t, :], PF[t][:, :], ALU.add).then_inc(S_de, 1)

                    def ffn(c):
                        return lambda slot: [ffn_step(c, *s) for s in ffn_slots[slot]]

                    nc.vector.memset(state[:, :, :], 0.0).then_inc(S_st0, 1)
                    nc.vector.memset(eps[:, :], EPS)
                    nc.vector.memset(neghalf[:, :], -0.5).then_inc(S_const, 1)
                    dve.wait_ge(S_w, 16 * 9)
                    dve.wait_ge(S_an, 1)
                    nc.vector.tensor_scalar(an[:, :, :], an[:, :, :], -1.0, None, ALU.mult).then_inc(S_an, 1)
                    nc.vector.tensor_scalar(gsh[:, :], wsg, 0.5 / D ** 0.5, None, ALU.mult).then_inc(S_cs, 1)
                    nc.vector.tensor_tensor(cs[:, :], wsg, wsu, ALU.mult).then_inc(S_cs, 1)
                    dve.wait_ge(S_cs, 2)
                    nc.vector.tensor_tensor(cs[:, :], cs[:, :], su_dp, ALU.mult).then_inc(S_cs, 1)
                    dve.wait_ge(S_cs, 3)
                    nc.vector.tensor_scalar(cs[:, :], cs[:, :], 0.5 / (D * F0 ** 0.5), None, ALU.mult).then_inc(S_cs, 1)
                    dve.wait_ge(S_st0, 1)
                    nc.vector.memset(fill[:, 0:ROW - 1], 0.0).then_inc(S_z, 1)
                    head(0, lambda slot: None)
                    for n in range(NS):
                        scan(0, n, lambda slot: None)
                    dve.wait_ge(S_bc, 4)
                    tail(0)
                    with dve.Fori(1, NCH) as c:
                        f = ffn(c - 1)
                        head(c, f)
                        for n in range(NS):
                            scan(c, n, f)
                        tail(c)
                    for slot in range(len(ffn_slots)):
                        ffn(NCH - 1)(slot)

                @block.gpsimd
                def _(pool):
                    def add(c, n):
                        i = NS * c + n
                        pool.wait_ge(S_cm, i + 1)
                        wait(pool, S_ya, i)
                        if n == 0:
                            pool.wait_ge(S_yi, c + 1)
                        nc.gpsimd.tensor_tensor(y[:, :, :], y[:, :, :], bx[n % 2][:, :, :], ALU.add).then_inc(S_ya, 1)

                    def butterfly(i, second):
                        lo, hi = ((0, 1), (2, 3), (0, 2), (1, 3))[i]
                        p, q = wdn[:, 4 * lo:4 * lo + 4, :], wdn[:, 4 * hi:4 * hi + 4, :]
                        if not second:
                            pool.wait_ge(S_pev, 16)
                            wait(pool, S_bc, i)
                            wait(pool, S_bf, 2 * i)
                            nc.gpsimd.tensor_tensor((x1, xn2T)[i % 2][:, :, :], p, q, ALU.add).then_inc(S_bf, 1)
                        else:
                            pool.wait_ge(S_bf, 2 * i + 1)
                            nc.gpsimd.tensor_tensor(q, p, q, ALU.subtract).then_inc(S_bf, 1)

                    pool.wait_ge(S_w, 16 * 9)
                    nc.gpsimd.iota(fill[:, ROW - 1:ROW], [[0, 1]], base=T, channel_multiplier=1,
                                   allow_small_or_imprecise_dtypes=True).then_inc(S_z, 1)
                    norm_rstd(pool, n1, 0)
                    for g in range(4):
                        pool.wait_ge(S_raw[g % 2], 16 * (g // 2 + 1))
                        nc.gpsimd.tensor_tensor(raw[g % 2], raw[g % 2], wsdp.unsqueeze(1).to_broadcast([P, 4, D]), ALU.mult).then_inc(S_wsc, 1)
                    for n in range(NS):
                        add(0, n)
                        if n >= 8:
                            butterfly((n - 8) // 2, n % 2 == 1)
                    norm_rstd(pool, n2, 0)
                    with pool.Fori(1, NCH) as c:
                        norm_rstd(pool, n1, c)
                        for n in range(NS):
                            add(c, n)
                        norm_rstd(pool, n2, c)

        B = ExitStack()
        with B:
            wx = sb(B, "wx", [P, 2, KT, I1], f32r)
            wz = sb(B, "wz", [P, 2, KT, I1], f32r)
            wo = sb(B, "wo", [P, 2, M1, D], f32r)
            gate = sb(B, "gate", [P, KT, E])
            dh = sb(B, "dh", [P, M1])
            before_f = sb(B, "before_f", [P, P])
            before = sb(B, "before", [P, P], bf16)
            ones = sb(B, "ones", [P, P], bf16)
            chosen_sum = sb(B, "chosen_sum", [P, E], bf16)
            first_slot = sb(B, "first_slot", [P, E])
            number = sb(B, "number", [P, 1])
            xb = sb(B, "xb", [P, TT, D])
            xr = sb(B, "xr", [P, TT, D])
            x3 = sb(B, "x3", [P, TT, D])
            xn3 = sb(B, "xn3", [P, 2, D])
            xT = sb(B, "xT", [P, 2, KT, CH], f32r)
            gm = sb(B, "gm", [P, 2, M1, CH], f32r)
            tz = sb(B, "tz", [P, 2, CH])
            row = sb(B, "row", [P, 2, ROW])
            x4T = sb(B, "x4T", [P, KT, P])
            rt = sb(B, "rt", [P, 8, E])
            rc = sb(B, "rc", [P, 8])
            top8 = sb(B, "top8", [P, 3, TOPK])
            chosen_b = sb(B, "chosen_b", [P, E], bf16)
            idx = sb(B, "idx", [P, 2, TOPK], u32)
            fx = sb(B, "fx", [P, TT, D])
            BZ, BX, BT, BO = bank[0:2], bank[2:4], bank[4:6], bank[6:8]

            n3, n4 = Norm("n3"), Norm("n4")
            S_w = sem("b_weights"); S_big = [sem("b_big0"), sem("b_big1")]; S_sm = sem("b_small")
            S_fm = sem("fold_mm"); S_fh = sem("fold_hi"); S_fl = sem("fold_lo"); S_wh = sem("weight_hi"); S_wl = sem("weight_lo")
            S_xb = sem("xb_in"); S_xr = sem("xr_in"); S_zm = sem("z_mm"); S_xm = sem("xc_mm"); S_tz = sem("z_tanh")
            S_zg = sem("z_gated"); S_gf = sem("g_made"); S_gh = sem("g_hi"); S_gl = sem("g_lo")
            S_om = sem("out_mm"); S_x3 = sem("x3_made"); S_st = sem("x3_stored")
            S_lg = sem("logits_mm"); S_r = sem("route_step"); S_ex = sem("route_exp"); S_pm = sem("place_mm")
            S_ix = sem("slot_ready"); S_sct = [sem("rows_out0"), sem("rows_out1")]
            RS = 17

            S_bt = sem("triangle_ready")

            stage, fold_in = [xb[:, :, :], xr[:, :, :]], [x3[:, :, :], fx[:, :, :]]
            conv, winz, wout = (a[n].rearrange("(k p) i -> p k i", p=P) for n in ("convT", "winzT", "woT"))
            pieces = [conv[:, 4 * q:4 * q + 4, h * 512:h * 512 + 512] for h in range(2) for q in range(2)] + \
                     [winz[:, :, h * 512:h * 512 + 512] for h in range(2)] + [wout[:, 4 * q:4 * q + 4, :] for q in range(2)]

            def plain(part, i):
                return wz[:, part, :, i * 512:i * 512 + 512] if i < 2 else wo[:, part, 4 * i - 8:4 * i - 4, :]

            with nc.Block() as block:

                @block.sync
                def _(sp):
                    for dst, src in ((gate[:, :, :], a["gateT"].rearrange("(k p) e -> p k e", p=P)), (dh[:, :], a["d1"]),
                                     (before_f[:, :], a["before"]), (first_slot[:, :], a["first_slot"]), (number[:, :], a["number"])):
                        sp.dma_start(dst, src).then_inc(S_sm, 16)
                    for q in range(2):
                        sp.dma_start(fold_in[q], a["winx"].rearrange("(k p) h -> p k h", p=P)[:, 4 * q:4 * q + 4, :]).then_inc(S_w, 16)
                    for i, src in enumerate(pieces):
                        if 2 <= i < 6:
                            sp.wait_ge(S_fm, KT * (i - 1))
                        if i >= 6:
                            sp.wait_ge(S_wl, i - 5)
                        sp.dma_start(stage[i % 2], src).then_inc(S_big[i % 2], 16)

                    def load(c):
                        sp.dma_start(xb[:, :, :], chunk(a["x2"], c)).then_inc(S_xb, 16)

                    sp.wait_ge(S_wl, 4)
                    load(0)
                    sp.dma_start(xr[:, :, :], chunk(a["x2"], 0)).then_inc(S_xr, 16)
                    sp.wait_ge(n3.xn, 4)
                    load(1)
                    for c in range(NCH):
                        sp.wait_ge(S_x3, 4 * c + 4)
                        sp.dma_start(chunk(acc[0], c), x3[:, :, :]).then_inc(S_st, 16)
                        if c + 1 < NCH:
                            sp.dma_start(xr[:, :, :], chunk(a["x2"], c + 1)).then_inc(S_xr, 16)
                        if c + 2 < NCH:
                            sp.wait_ge(n3.xn, 4 * c + 8)
                            load(c + 2)
                    sp.wait_ge(S_st, 16 * NCH)

                def split3(out, w_of, x_of, n):
                    for k in range(n):
                        for wp, xp in ((0, 0), (1, 0), (0, 1)):
                            last = nc.tensor.matmul(out, w_of(wp, k), x_of(xp, k), start=(k == 0 and wp == 0 and xp == 0),
                                                    stop=(k == n - 1 and xp == 1))
                    return last

                @block.tensor
                def _(pe):
                    def norm_T(n, c, t, src):
                        pe.wait_ge(n.xn, 4 * c + t + 1)
                        for k in range(KT):
                            last = nc.tensor.transpose(BT[t % 2][:, k * P:(k + 1) * P], src(t)[:, k * P:(k + 1) * P], ident[:, :])
                        last.then_inc(n.tp, 1)

                    def norm3(c, t):
                        if t >= 2:
                            pe.wait_ge(n3.lo, 4 * c + t - 1)
                        norm_T(n3, c, t, lambda t: xn3[:, t % 2, :])

                    def mixer(c, m):
                        if m == 0:
                            pe.wait_ge(n3.lo, 4 * c + 4)
                        if m >= 2:
                            pe.wait_ge(S_gf, M1 * c + m - 1)
                        for b, w, s in ((BZ[m % 2], wz, S_zm), (BX[m % 2], wx, S_xm)):
                            split3(b[:, :], lambda q, k: w[:, q, k, m * P:(m + 1) * P], lambda q, k: xT[:, q, k, :], KT).then_inc(s, 1)

                    def out(c, t):
                        if t == 0:
                            pe.wait_ge(S_gl, M1 * (c + 1))
                        if t >= 2:
                            pe.wait_ge(S_x3, 4 * c + t - 1)
                        split3(BO[t % 2][:, :], lambda q, k: gm[:, q, k, t * P:(t + 1) * P],
                               lambda q, k: wo[:, q, k, :], M1).then_inc(S_om, 1)

                    def route_T(c, t):
                        norm_T(n4, c, t, lambda t: row[:, t % 2, 0:D])

                    def logits(c, t):
                        pe.wait_ge(n4.xT, 4 * c + t + 1)
                        for k in range(KT):
                            last = nc.tensor.matmul(BO[0][:, 0:E], x4T[:, k, :], gate[:, k, :], start=(k == 0), stop=(k == KT - 1))
                        last.then_inc(S_lg, 1)

                    def place(c, t):
                        pe.wait_ge(S_r, RS * (4 * c + t) + 10)
                        nc.tensor.matmul(BO[1][:, 0:E], before[:, :], chosen_b[:, :], start=True, stop=False)
                        nc.tensor.matmul(BO[1][:, 0:E], ones[:, :], chosen_sum[:, :], start=False, stop=True).then_inc(S_pm, 1)

                    pe.wait_ge(S_w, 32)
                    for half in range(2):
                        for q in range(2):
                            i = 2 * half + q
                            pe.wait_ge(S_big[i % 2], 16 * (i // 2 + 1))
                            if q == 0 and half == 1:
                                pe.wait_ge(S_fl, KT)
                            for m in range(KT):
                                for k in range(4):
                                    last = nc.tensor.matmul(bank[m][:, :], fold_in[q][:, k, m * P:(m + 1) * P], stage[i % 2][:, k, :],
                                                            start=(k == 0 and q == 0), stop=(k == 3 and q == 1))
                                last.then_inc(S_fm, 1)
                    pe.wait_ge(S_fl, 2 * KT)
                    pe.wait_ge(S_wl, 4)
                    for t in range(TT):
                        norm3(0, t)

                    def body(c, routing, following):
                        for m in range(M1):
                            mixer(c, m)
                            if routing and m % 2 == 0:
                                route_T(c - 1, m // 2)
                                if m:
                                    place(c - 1, m // 2 - 1)
                            if routing and m % 2 == 1:
                                logits(c - 1, m // 2)
                        if routing:
                            place(c - 1, TT - 1)
                            pe.wait_ge(S_r, RS * 4 * c)
                        for t in range(TT):
                            out(c, t)
                            if following:
                                norm3(c + 1, t)

                    for c in range(NCH):
                        body(c, c > 0, c + 1 < NCH)
                    for t in range(TT):
                        route_T(NCH - 1, t)
                        logits(NCH - 1, t)
                        place(NCH - 1, t)

                @block.scalar
                def _(act):
                    def split_hi(c, t):
                        act.wait_ge(n3.tp, 4 * c + t + 1)
                        nc.scalar.activation(xT[:, 0, :, t * P:(t + 1) * P], BT[t % 2][:, :].rearrange("p (k q) -> p k q", k=KT),
                                             ACT.Copy).then_inc(n3.xT, 1)

                    def mixer(c, m):
                        act.wait_ge(S_zm, M1 * c + m + 1)
                        if m >= 2:
                            act.wait_ge(S_gl, M1 * c + m - 1)
                        else:
                            wait(act, S_gl, M1 * c)
                        nc.scalar.activation(tz[:, m % 2, :], BZ[m % 2][:, :], ACT.Tanh, scale=0.5).then_inc(S_tz, 1)

                    def g_hi(c, m):
                        act.wait_ge(S_gf, M1 * c + m + 1)
                        nc.scalar.activation(gm[:, 0, m, :], tz[:, m % 2, :], ACT.Copy).then_inc(S_gh, 1)

                    def route_T(c, t):
                        act.wait_ge(n4.tp, 4 * c + t + 1)
                        nc.scalar.activation(x4T[:, :, :], BT[t % 2][:, :].rearrange("p (k q) -> p k q", k=KT), ACT.Copy).then_inc(n4.xT, 1)

                    def route_exp(c, t):
                        act.wait_ge(S_r, RS * (4 * c + t) + 2)
                        nc.scalar.activation(rt[:, 0, :], BO[0][:, 0:E], ACT.Exp, bias=rc[:, 1:2], accum_out=rc[:, 2:3]).then_inc(S_ex, 1)

                    for half in range(2):
                        for m in range(KT):
                            act.wait_ge(S_fm, KT * (2 * half + 1) + m + 1)
                            nc.scalar.activation(wx[:, 0, m, half * 512:half * 512 + 512], bank[m][:, :], ACT.Copy).then_inc(S_fh, 1)
                    for i in range(4):
                        act.wait_ge(S_big[i % 2], 16 * (i // 2 + 3))
                        nc.scalar.activation(plain(0, i), stage[i % 2], ACT.Copy).then_inc(S_wh, 1)
                    for t in range(TT):
                        split_hi(0, t)

                    def body(c, routing, following):
                        for m in range(M1):
                            mixer(c, m)
                            g_hi(c, m)
                            if routing:
                                (route_exp if m % 2 else route_T)(c - 1, m // 2)
                        if following:
                            for t in range(TT):
                                split_hi(c + 1, t)

                    for c in range(NCH):
                        body(c, c > 0, c + 1 < NCH)
                    for t in range(TT):
                        route_T(NCH - 1, t)
                        route_exp(NCH - 1, t)

                @block.vector
                def _(dve):
                    def norm3(c):
                        dve.wait_ge(S_xb, 16 * (c + 1))
                        norm_stats(dve, n3, c, xb)
                        dve.wait_ge(n3.rs, c + 1)

                    def norm3_tile(c, t):
                        if t >= 2:
                            dve.wait_ge(n3.tp, 4 * c + t - 1)
                        normalize(n3, t, xn3[:, t % 2, :], xb)

                    def split_lo(c, t):
                        dve.wait_ge(n3.xT, 4 * c + t + 1)
                        hi = xT[:, 0, :, t * P:(t + 1) * P]
                        nc.vector.tensor_tensor(xT[:, 1, :, t * P:(t + 1) * P], BT[t % 2][:, :].rearrange("p (k q) -> p k q", k=KT),
                                                hi.bitcast(fp32), ALU.subtract).then_inc(n3.lo, 1)

                    def mixer(c, m):
                        dve.wait_ge(S_tz, M1 * c + m + 1)
                        nc.vector.scalar_tensor_tensor(out=tz[:, m % 2, :], in0=tz[:, m % 2, :], scalar=1.0, in1=BZ[m % 2][:, :],
                                                       op0=ALU.add, op1=ALU.mult).then_inc(S_zg, 1)
                        dve.wait_ge(S_xm, M1 * c + m + 1)
                        dve.wait_ge(S_zg, M1 * c + m + 1)
                        nc.vector.scalar_tensor_tensor(out=tz[:, m % 2, :], in0=BX[m % 2][:, :], scalar=dh[:, m:m + 1],
                                                       in1=tz[:, m % 2, :], op0=ALU.mult, op1=ALU.mult).then_inc(S_gf, 1)
                        dve.wait_ge(S_gh, M1 * c + m + 1)
                        nc.vector.tensor_tensor(gm[:, 1, m, :], tz[:, m % 2, :], gm[:, 0, m, :].bitcast(fp32), ALU.subtract).then_inc(S_gl, 1)

                    def out(c, t):
                        dve.wait_ge(S_om, 4 * c + t + 1)
                        if t == 0:
                            dve.wait_ge(S_xr, 16 * (c + 1))
                            wait(dve, S_st, 16 * c)
                        nc.vector.tensor_tensor(x3[:, t, :], xr[:, t, :], BO[t % 2][:, :], ALU.add).then_inc(S_x3, 1)

                    def norm4(c):
                        dve.wait_ge(S_x3, 4 * c + 4)
                        norm_stats(dve, n4, c, x3)
                        dve.wait_ge(n4.rs, c + 1)

                    def route(c, t, part):
                        i = 4 * c + t
                        r = row[:, t % 2, :]
                        pr, rest, chosen, key, v = (rt[:, j, :] for j in range(1, 6))

                        def after(s):
                            dve.wait_ge(S_const, 1)
                            dve.wait_ge(S_r, RS * i + s)

                        if part == 0:
                            wait(dve, S_sct[t % 2], 16 * TOPK * (2 * c + t // 2))
                            normalize(n4, t, r[:, 0:D], x3)
                        elif part == 1:
                            nc.vector.tensor_copy(r[:, ROW - 1:ROW], number[:, :])
                            dve.wait_ge(S_lg, i + 1)
                            nc.vector.reduce_max(rc[:, 0:1], BO[0][:, 0:E], AX.X).then_inc(S_r, 1)
                            after(1)
                            nc.vector.tensor_scalar(rc[:, 1:2], rc[:, 0:1], -1.0, None, ALU.mult).then_inc(S_r, 1)
                            after(2)
                            nc.vector.tensor_scalar(number[:, :], number[:, :], float(P), None, ALU.add).then_inc(S_r, 1)
                            dve.wait_ge(S_ex, i + 1)
                            nc.vector.reciprocal(rc[:, 3:4], rc[:, 2:3]).then_inc(S_r, 1)
                            after(4)
                            nc.vector.tensor_scalar(pr, rt[:, 0, :], rc[:, 3:4], None, ALU.mult).then_inc(S_r, 1)
                            after(5)
                            nc.vector.max(top8[:, 0, :], pr).then_inc(S_r, 1)
                            after(6)
                            nc.vector.match_replace(rest, top8[:, 0, :], pr, -1.0).then_inc(S_r, 1)
                            after(7)
                            nc.vector.tensor_scalar(chosen, rest, 0.0, None, ALU.is_lt).then_inc(S_r, 1)
                            nc.vector.reduce_sum(rc[:, 4:5], top8[:, 0, :], AX.X).then_inc(S_r, 1)
                            after(8)
                            nc.vector.tensor_copy(chosen_b[:, :], chosen).then_inc(S_r, 1)
                            after(9)
                            nc.vector.reciprocal(rc[:, 5:6], rc[:, 4:5]).then_inc(S_r, 1)
                        else:
                            after(11)
                            nc.vector.scalar_tensor_tensor(out=r[:, D:D + E], in0=pr, scalar=rc[:, 5:6], in1=chosen,
                                                           op0=ALU.mult, op1=ALU.mult).then_inc(S_r, 1)
                            dve.wait_ge(S_pm, i + 1)
                            nc.vector.tensor_tensor(chosen_sum[:, :], chosen_sum[:, :], chosen_b[:, :], ALU.add)
                            nc.vector.tensor_tensor(key, BO[1][:, 0:E], first_slot[:, :], ALU.add)
                            nc.vector.scalar_tensor_tensor(out=v, in0=BO[1][:, 0:E], scalar=float(CAP), in1=chosen,
                                                           op0=ALU.is_lt, op1=ALU.mult).then_inc(S_r, 1)
                            after(13)
                            nc.vector.tensor_tensor(key, key, v, ALU.mult).then_inc(S_r, 1)
                            after(14)
                            nc.vector.max(top8[:, 1, :], key).then_inc(S_r, 1)
                            after(15)
                            nc.vector.tensor_scalar(top8[:, 2, :], top8[:, 1, :], 0.0, FAR, ALU.is_equal, ALU.mult).then_inc(S_r, 1)
                            after(16)
                            nc.vector.scalar_tensor_tensor(out=idx[:, t % 2, :], in0=top8[:, 1, :], scalar=-1.0, in1=top8[:, 2, :],
                                                           op0=ALU.add, op1=ALU.add).then_inc(S_r, 1)

                    dve.wait_ge(S_sm, 80)
                    nc.vector.memset(ones[:, :], 1.0)
                    nc.vector.memset(chosen_sum[:, :], 0.0)
                    nc.vector.tensor_scalar(dh[:, :], dh[:, :], 0.5, None, ALU.mult)
                    nc.vector.tensor_copy(before[:, :], before_f[:, :]).then_inc(S_bt, 1)
                    for half in range(2):
                        for m in range(KT):
                            dve.wait_ge(S_fh, KT * half + m + 1)
                            cols = slice(half * 512, half * 512 + 512)
                            last = nc.vector.tensor_tensor(wx[:, 1, m, cols], bank[m][:, :], wx[:, 0, m, cols].bitcast(fp32), ALU.subtract)
                            last.then_inc(S_fl, 1)
                    for i in range(4):
                        dve.wait_ge(S_wh, i + 1)
                        nc.vector.tensor_tensor(plain(1, i), stage[i % 2], plain(0, i).bitcast(fp32), ALU.subtract).then_inc(S_wl, 1)
                    norm3(0)
                    for t in range(TT):
                        norm3_tile(0, t)
                        if t >= 1:
                            split_lo(0, t - 1)
                    split_lo(0, TT - 1)

                    def body(c, routing, following):
                        if routing:
                            norm4(c - 1)
                        for m in range(M1):
                            if routing and m % 2 == 0:
                                route(c - 1, m // 2, 0)
                            mixer(c, m)
                            if routing and m % 2 == 1:
                                route(c - 1, m // 2, 1)
                            if routing and m % 2 == 0 and m:
                                route(c - 1, m // 2 - 1, 2)
                        if routing:
                            route(c - 1, TT - 1, 2)
                        if following:
                            norm3(c + 1)
                        for t in range(TT):
                            out(c, t)
                            if following:
                                norm3_tile(c + 1, t)
                                if t >= 1:
                                    split_lo(c + 1, t - 1)
                        if following:
                            split_lo(c + 1, TT - 1)

                    for c in range(NCH):
                        body(c, c > 0, c + 1 < NCH)
                    norm4(NCH - 1)
                    for t in range(TT):
                        for part in range(3):
                            route(NCH - 1, t, part)

                @block.gpsimd
                def _(pool):
                    def rows_out(c, t):
                        pool.wait_ge(S_const, 1)
                        pool.wait_ge(S_r, RS * (4 * c + t + 1))
                        for k in range(TOPK):
                            nc.gpsimd.indirect_dma_start(a["slots"][:, :], bass.IndirectOffsetOnAxis(idx[:, t % 2, k:k + 1], 0),
                                                         row[:, t % 2, :], None, bounds_check=E * P - 1, oob_is_err=False).then_inc(S_sct[t % 2], 16)

                    norm_rstd(pool, n3, 0)
                    for c in range(NCH + 1):
                        if c >= 1:
                            norm_rstd(pool, n4, c - 1)
                            for t in range(TT):
                                rows_out(c - 1, t)
                        if c + 1 < NCH:
                            norm_rstd(pool, n3, c + 1)
                    for s in S_sct:
                        pool.wait_ge(s, 16 * TOPK * 2 * NCH)

        C = ExitStack()
        with C:
            xe = sb(C, "xe", [P, SLOTS, ROW])
            wgu = sb(C, "wgu", [P, SLOTS, KT, 2 * FE])
            wde = sb(C, "wde", [FH, SLOTS, 2, D])
            xeT = sb(C, "xeT", [P, 2, KT, P])
            te = sb(C, "te", [P, 2, FE])
            he = sb(C, "he", [P, 2, FE])
            hT = sb(C, "hT", [FH, 2, 2, P])
            ye = sb(C, "ye", [P, 2, D])
            wsc = sb(C, "wsc", [P, 2])
            tok = sb(C, "tok", [P, 2], u32)
            CX, CG, CH_, CO = bank[0:2], bank[2:4], bank[4:6], bank[6:8]
            S_xe = [sem(f"rows_in{i}") for i in range(SLOTS)]
            S_gu = [sem(f"gate_up_in{i}") for i in range(SLOTS)]
            S_dn = [sem(f"down_in{i}") for i in range(SLOTS)]
            S_xt = sem("rows_transposed"); S_xc = sem("rows_copied"); S_gm = sem("gate_up_mm"); S_et = sem("e_tanh")
            S_eg = sem("e_half_gated"); S_h = sem("h_made"); S_ht = sem("h_transposed"); S_hc = sem("h_copied")
            S_y = sem("down_e_mm"); S_ws = sem("slot_weights"); S_ys = sem("rows_scaled"); S_add = [sem("added0"), sem("added1")]

            with nc.Block() as block:
                def rounds(eng, f):
                    for i in range(SLOTS):
                        f(0, i)
                    with eng.Fori(1, E // SLOTS) as q:
                        for i in range(SLOTS):
                            f(q, i)

                @block.sync
                def _(sp):
                    def load(q, i):
                        e = SLOTS * q + i
                        first = isinstance(q, int) and q == 0
                        if not first:
                            sp.wait_ge(S_ws, e - SLOTS + 1)
                            sp.wait_ge(S_gm, e - SLOTS + 1)
                        sp.dma_start(xe[:, i, :], a["slots"][ds(e * P, P), :]).then_inc(S_xe[i], 16)
                        for w, off in ((a["wg"], 0), (a["wu"], FE)):
                            sp.dma_start(wgu[:, i, :, off:off + FE], w.rearrange("e h f -> (e h) f")[ds(e * D, D), :]
                                         .rearrange("(k p) f -> p k f", p=P)).then_inc(S_gu[i], 16)
                        if not first:
                            sp.wait_ge(S_y, e - SLOTS + 1)
                        sp.dma_start(wde[:, i, :, :], a["wd"].rearrange("e f h -> (e f) h")[ds(e * FE, FE), :]
                                     .rearrange("(s p) h -> p s h", p=FH)).then_inc(S_dn[i], 16)
                    rounds(sp, load)

                @block.tensor
                def _(pe):
                    def up(q, i):
                        e = SLOTS * q + i
                        pe.wait_ge(S_xe[i], 16 * (q + 1))
                        wait(pe, S_xc, e - 1)
                        for k in range(KT):
                            last = nc.tensor.transpose(CX[i % 2][:, k * P:(k + 1) * P], xe[:, i, k * P:(k + 1) * P], ident[:, :])
                        last.then_inc(S_xt, 1)
                        pe.wait_ge(S_gu[i], 32 * (q + 1))
                        pe.wait_ge(S_xc, e + 1)
                        wait(pe, S_h, e - 1)
                        for k in range(KT):
                            last = nc.tensor.matmul(CG[i % 2][:, 0:2 * FE], xeT[:, i % 2, k, :], wgu[:, i, k, :],
                                                    start=(k == 0), stop=(k == KT - 1))
                        last.then_inc(S_gm, 1)

                    def down(q, i):
                        e = SLOTS * q + i
                        pe.wait_ge(S_h, e + 1)
                        wait(pe, S_hc, e - 1)
                        for s in range(2):
                            last = nc.tensor.transpose(CH_[i % 2][0:FH, s * P:(s + 1) * P], he[:, i % 2, s * FH:(s + 1) * FH], ident[:, :])
                        last.then_inc(S_ht, 1)
                        pe.wait_ge(S_dn[i], 16 * (q + 1))
                        pe.wait_ge(S_hc, e + 1)
                        wait(pe, S_ys, e - 1)
                        for s in range(2):
                            last = nc.tensor.matmul(CO[i % 2][:, :], hT[:, i % 2, s, :], wde[:, i, s, :], start=(s == 0), stop=(s == 1))
                        last.then_inc(S_y, 1)

                    def before_(q, i):
                        return (q, i - 1) if i else (q - 1, SLOTS - 1)

                    up(0, 0)
                    for i in range(1, SLOTS):
                        up(0, i)
                        down(0, i - 1)
                    with pe.Fori(1, E // SLOTS) as q:
                        for i in range(SLOTS):
                            up(q, i)
                            down(*before_(q, i))
                    down(E // SLOTS - 1, SLOTS - 1)

                @block.scalar
                def _(act):
                    def up(q, i):
                        e = SLOTS * q + i
                        act.wait_ge(S_xt, e + 1)
                        wait(act, S_gm, e - 1)
                        nc.scalar.activation(xeT[:, i % 2, :, :], CX[i % 2][:, :].rearrange("p (k q) -> p k q", k=KT), ACT.Copy).then_inc(S_xc, 1)
                        act.wait_ge(S_gm, e + 1)
                        wait(act, S_h, e - 1)
                        nc.scalar.activation(te[:, i % 2, :], CG[i % 2][:, 0:FE], ACT.Tanh, scale=0.5).then_inc(S_et, 1)

                    def down(q, i):
                        e = SLOTS * q + i
                        act.wait_ge(S_y, e + 1)
                        act.wait_ge(S_ws, e + 1)
                        if isinstance(q, int) and q == 0:
                            if i >= 2:
                                act.wait_ge(S_add[i % 2], 16)
                        else:
                            act.wait_ge(S_add[i % 2], 16 * (2 * q + i // 2))
                        nc.scalar.activation(ye[:, i % 2, :], CO[i % 2][:, :], ACT.Copy, scale=wsc[:, i % 2:i % 2 + 1]).then_inc(S_ys, 1)

                    up(0, 0)
                    for i in range(1, SLOTS):
                        up(0, i)
                        down(0, i - 1)
                    with act.Fori(1, E // SLOTS) as q:
                        for i in range(SLOTS):
                            up(q, i)
                            down(*((q, i - 1) if i else (q - 1, SLOTS - 1)))
                    down(E // SLOTS - 1, SLOTS - 1)

                @block.vector
                def _(dve):
                    def gated(q, i):
                        e = SLOTS * q + i
                        dve.wait_ge(S_xe[i], 16 * (q + 1))
                        wait(dve, S_ys, e - 1)
                        if isinstance(q, int) and q == 0:
                            if i >= 2:
                                dve.wait_ge(S_add[i % 2], 16)
                        else:
                            dve.wait_ge(S_add[i % 2], 16 * (2 * q + i // 2))
                        nc.vector.tensor_scalar(wsc[:, i % 2:i % 2 + 1], xe[:, i, ds(D + e, 1)], 0.5, None, ALU.mult)
                        nc.vector.tensor_copy(tok[:, i % 2:i % 2 + 1], xe[:, i, ROW - 1:ROW]).then_inc(S_ws, 1)
                        dve.wait_ge(S_et, e + 1)
                        nc.vector.scalar_tensor_tensor(out=te[:, i % 2, :], in0=te[:, i % 2, :], scalar=1.0, in1=CG[i % 2][:, 0:FE],
                                                       op0=ALU.add, op1=ALU.mult).then_inc(S_eg, 1)
                        wait(dve, S_ht, e - 1)
                        dve.wait_ge(S_eg, e + 1)
                        nc.vector.tensor_tensor(he[:, i % 2, :], te[:, i % 2, :], CG[i % 2][:, FE:2 * FE], ALU.mult).then_inc(S_h, 1)

                    def copy_T(q, i):
                        e = SLOTS * q + i
                        dve.wait_ge(S_ht, e + 1)
                        wait(dve, S_y, e - 1)
                        nc.vector.tensor_copy(hT[:, i % 2, :, :], CH_[i % 2][0:FH, 0:2 * P].rearrange("p (s q) -> p s q", s=2)).then_inc(S_hc, 1)

                    gated(0, 0)
                    for i in range(1, SLOTS):
                        copy_T(0, i - 1)
                        gated(0, i)
                    with dve.Fori(1, E // SLOTS) as q:
                        for i in range(SLOTS):
                            copy_T(*((q, i - 1) if i else (q - 1, SLOTS - 1)))
                            gated(q, i)
                    copy_T(E // SLOTS - 1, SLOTS - 1)

                @block.gpsimd
                def _(pool):
                    for e in range(E):
                        pool.wait_ge(S_ys, e + 1)
                        wait(pool, S_add[e % 2], 16 * (e // 2))
                        nc.gpsimd.indirect_dma_start(acc[e % 2][:, :], bass.IndirectOffsetOnAxis(tok[:, e % 2:e % 2 + 1], 0),
                                                     ye[:, e % 2, :], None, bounds_check=NROWS - 1, compute_op=ALU.add).then_inc(S_add[e % 2], 16)
                    for s in S_add:
                        pool.wait_ge(s, 16 * E // 2)

        Dd = ExitStack()
        with Dd:
            pa = sb(Dd, "pa", [P, NCH, TT, D])
            pb_ = sb(Dd, "pb", [P, NCH, TT, D])
            S_ab = [sem(f"sums_in{c}") for c in range(NCH)]
            S_s = sem("summed"); S_out = sem("out_stored")
            with nc.Block() as block:
                @block.sync
                def _(sp):
                    for c in range(NCH):
                        sp.dma_start(pa[:, c], chunk(acc[0], c)).then_inc(S_ab[c], 16)
                        sp.dma_start(pb_[:, c], chunk(acc[1], c)).then_inc(S_ab[c], 16)
                    for c in range(NCH):
                        sp.wait_ge(S_s, c + 1)
                        sp.dma_start(chunk(a["out"][0], c), pa[:, c]).then_inc(S_out, 16)
                    sp.wait_ge(S_out, 16 * NCH)

                @block.vector
                def _(dve):
                    for c in range(NCH):
                        dve.wait_ge(S_ab[c], 32)
                        nc.vector.tensor_tensor(pa[:, c], pa[:, c], pb_[:, c], ALU.add).then_inc(S_s, 1)


def arrange(i):
    g = {k: np.asarray(v) for k, v in i.items()}
    cols = lambda v: v.reshape(-1, P).T
    m = {
        "x": g["L0_attn_x"],
        "wxpT": g["L0_attn_W_xproj"].T, "wdtT": g["L0_attn_W_dt"].T, "A_log": g["L0_attn_A_log"],
        "vec": np.concatenate([cols(g["L0_attn_b_dt"]), cols(g["L0_attn_D_param"]), cols(g["L0_ffn_SU_ug"]),
                               cols(g["L0_ffn_SU_dp"]), cols(g["L0_ffn_Wscale_ug"][F0:]), cols(g["L0_ffn_Wscale_ug"][:F0])], 1),
        "ws_dp": g["L0_ffn_Wscale_dp"],
        "wuT": g["L0_ffn_W_up"].T, "wgT": g["L0_ffn_W_gate"].T, "wdT": g["L0_ffn_W_down"].T,
        "winx": g["L1_attn_W_in"][:I1], "winzT": g["L1_attn_W_in"][I1:].T,
        "convT": g["L1_attn_conv_w"].T, "d1": cols(g["L1_attn_D"]), "woT": g["L1_attn_W_out"].T,
        "gateT": g["L1_ffn_gate_w"].T, "wg": g["L1_ffn_wg"], "wu": g["L1_ffn_wu"], "wd": g["L1_ffn_wd"],
    }
    h = hadamard(P).astype(np.float32)
    sel = np.zeros((P, 2 * NS), np.float32)
    for n in range(2 * NS):
        sel[R + n, n] = sel[R + 2 * NS + n, n] = 1
    m["ident"] = np.eye(P, dtype=np.float32)
    m["had"] = np.concatenate([h, -h], 1)
    m["sel"] = sel
    m["before"] = np.triu(np.ones((P, P), np.float32), 1)
    m["first_slot"] = np.broadcast_to((np.arange(E) * P + 1).astype(np.float32), (P, E))
    m["number"] = np.arange(P, dtype=np.float32).reshape(P, 1)
    return {k: np.ascontiguousarray(v) for k, v in m.items()}


def kernel(**inputs):
    import concourse.bacc as bacc
    from concourse import mybir
    from concourse.bass_utils import run_bass_kernel_spmd

    nc = bacc.Bacc("TRN2", target_bir_lowering=False, num_devices=1, dynamic_dma_scratch_size=8192)
    arrays = arrange(inputs)
    a = {k: nc.dram_tensor(k + "_in", v.shape, mybir.dt.from_np(v.dtype), kind="ExternalInput").ap() for k, v in arrays.items()}
    for name, shape in (("x2", (T, D)), ("acc0", (NROWS, D)), ("acc1", (NROWS, D)), ("slots", (E * P, ROW))):
        a[name] = nc.dram_tensor(name, shape, mybir.dt.float32, kind="Internal").ap()
    a["out"] = nc.dram_tensor("out", (1, T, D), mybir.dt.float32, kind="ExternalOutput").ap()
    build(nc, a)
    r = run_bass_kernel_spmd(nc, [{k + "_in": v for k, v in arrays.items()}], core_ids=[0])
    return r.results[0]["out"]
```

```python
import numpy as np

T, D = 2048, 512
P = 128
CH = 512
NCH = T // CH
TT = CH // P
KT = D // P
NS = 16
R = 64
F0 = 2048
M0 = F0 // P
HALF = M0 // 2
I1 = 1024
M1 = I1 // P
E, TOPK, CAP, FE = 64, 8, 128, 192
FH = FE // 2
ROW = D + E + 1
NROWS = T + P
FAR = 1.0e6
EPS = 1e-5
RING = 3
SLOTS = 4


def hadamard(n):
    i = np.arange(n)
    v = i[:, None] & i[None, :]
    odd = np.zeros((n, n), np.int64)
    for b in range(n.bit_length()):
        odd += (v >> b) & 1
    return np.where(odd % 2, -1.0, 1.0)


H4 = hadamard(4).astype(int)


def build(nc, a):
    import concourse.bass as bass
    from concourse import mybir
    from contextlib import ExitStack

    fp32, f32r, bf16, u32 = mybir.dt.float32, mybir.dt.float32r, mybir.dt.bfloat16, mybir.dt.uint32
    ALU, ACT, AX = mybir.AluOpType, mybir.ActivationFunctionType, mybir.AxisListType
    ds = bass.ds
    top = ExitStack()
    sem = lambda n: top.enter_context(nc.semaphore(n))

    def wait(eng, s, v):
        if not (isinstance(v, int) and v <= 0):
            eng.wait_ge(s, v)

    def sb(ctx, name, shape, dt=fp32):
        return ctx.enter_context(nc.sbuf_tensor(name, shape, dt))

    def chunk(tensor, c):
        return tensor[ds(c * CH, CH), :].rearrange("(t p) d -> p t d", p=P)

    acc = [a["acc0"], a["acc1"]]

    class Norm:

        def __init__(self, n):
            self.bn = sem(n + "_bn")
            self.mv = sem(n + "_mv")
            self.ve = sem(n + "_ve")
            self.rs = sem(n + "_rs")
            self.xn = sem(n + "_xn")
            self.tp = sem(n + "_tp")
            self.xT = sem(n + "_xT")
            self.lo = sem(n + "_lo")

    with top:
        S_const = sem("constants_ready")
        small = top.enter_context(ExitStack())
        ident = sb(small, "ident", [P, P])
        st6 = sb(small, "st6", [P, TT, 6])
        mv = sb(small, "mv", [P, TT, 2])
        ve = sb(small, "ve", [P, TT])
        rs = sb(small, "rs", [P, TT])
        neghalf = sb(small, "neghalf", [P, TT])
        eps = sb(small, "eps", [P, TT])
        bank = [top.enter_context(nc.psum_tensor(f"bank{i}", [P, 512], fp32)) for i in range(8)]

        def norm_stats(dve, n, c, src):
            for t in range(TT):
                last = nc.vector.bn_stats(st6[:, t, :], src[:, t, :])
            last.then_inc(n.bn, 1)
            dve.wait_ge(S_const, 1)
            dve.wait_ge(n.bn, c + 1)
            for t in range(TT):
                last = nc.vector.bn_aggr(mv[:, t, :], st6[:, t, :])
            last.then_inc(n.mv, 1)

        def norm_rstd(pool, n, c):
            pool.wait_ge(S_const, 1)
            pool.wait_ge(n.mv, c + 1)
            nc.gpsimd.tensor_tensor(ve[:, :], mv[:, :, 1], eps[:, :], ALU.add).then_inc(n.ve, 1)
            pool.wait_ge(n.ve, c + 1)
            nc.gpsimd.tensor_tensor(rs[:, :], ve[:, :], neghalf[:, :], ALU.pow).then_inc(n.rs, 1)

        def normalize(n, t, dst, src):
            return nc.vector.tensor_scalar(dst, src[:, t, :], mv[:, t, 0:1], rs[:, t:t + 1],
                                           ALU.subtract, ALU.mult).then_inc(n.xn, 1)

        A = ExitStack()
        with A:
            wug = sb(A, "wug", [P, KT, 2 * F0], f32r)
            ring = sb(A, "ring", [P, RING, 2 * D], f32r)
            had = sb(A, "had", [P, 2, P])
            wxp = sb(A, "wxp", [P, KT, P])
            wdt = sb(A, "wdt", [R, D])
            sel = sb(A, "sel", [P, 2 * NS], f32r)
            self32 = sb(A, "self32", [P, 2 * NS])
            vec = sb(A, "vec", [P, 3 * KT + 3 * M0])
            b_dt, dpar, su_ug = vec[:, 0:KT], vec[:, KT:2 * KT], vec[:, 2 * KT:3 * KT]
            o = 3 * KT
            su_dp, wsg, wsu = (vec[:, o + i * M0:o + (i + 1) * M0] for i in range(3))
            an = sb(A, "an", [P, KT, NS])
            gsh = sb(A, "gsh", [P, M0])
            cs = sb(A, "cs", [P, M0])
            state = sb(A, "state", [P, KT, NS])
            xin = sb(A, "xin", [P, TT, D])
            xnt = sb(A, "xnt", [P, 2, D])
            y = sb(A, "y", [P, KT, CH])
            dl = sb(A, "dl", [P, KT, CH])
            u = sb(A, "u", [P, KT, CH])
            dA = [sb(A, f"dA{i}", [P, KT, CH]) for i in range(2)]
            bx = [sb(A, f"bx{i}", [P, KT, CH]) for i in range(2)]
            dtr = xnt[0:R, 0, :]
            xdr = sb(A, "xdr", [P, CH], f32r)
            x1 = sb(A, "x1", [P, TT, D])
            wsdp = x1[:, TT - 1, :]
            th = sb(A, "th", [P, 2, CH])
            with ExitStack() as prep_only:
                raw_u = sb(prep_only, "raw_u", [P, 2, 4, 512])
                raw_d = sb(prep_only, "raw_d", [P, 2, M0 * P])
                staged = sb(prep_only, "staged", [P, 8, 512], f32r)
            raw = [raw_u[:, i, :, :] for i in range(2)]
            rawd, sums = raw_d[:, 0, :], raw_d[:, 1, :]
            stage_u = [staged[:, i, :] for i in range(4)]
            stage_d = [[staged[:, 4 + 2 * i + part, :] for part in range(2)] for i in range(2)]
            xn2T = sb(A, "xn2T", [P, 2, KT, CH], f32r)
            act8 = sb(A, "act8", [P, 2, HALF, CH], f32r)
            PB, PC, PF = bank[0:2], bank[2:4], bank[4:8]
            HB = bank[0:4]

            n1, n2 = Norm("n1"), Norm("n2")
            S_x = sem("x_in"); S_w = sem("weights_in")
            S_raw = [sem("raw_in0"), sem("raw_in1")]; S_rawd = sem("raw_down_in")
            S_wsc = sem("raw_scaled"); S_pmm = sem("prep_mm"); S_ph = sem("prep_hi"); S_pl = sem("prep_lo")
            S_bf = sem("butterfly"); S_sel = sem("selectors")
            S_su = [sem(f"up_stored{i}") for i in range(4)]; S_sd = [sem(f"down_stored{i}") for i in range(2)]
            S_ring = [sem(f"ring_in{i}") for i in range(RING)]; S_dk = sem("down_block_used")
            S_an = sem("decay_rates"); S_cs = sem("scales_ready"); S_st0 = sem("state_zeroed")
            S_xd = sem("xdbl_mm"); S_hi = sem("xdbl_hi"); S_h2 = sem("xdbl_split"); S_dt = sem("dt_mm")
            S_abs = sem("sp_abs"); S_exp = sem("sp_exp"); S_ln = sem("sp_ln"); S_rel = sem("sp_relu")
            S_sp = sem("sp_sum"); S_dl = sem("delta_ready"); S_u = sem("u_ready"); S_yi = sem("y_init")
            S_bb = sem("b_bcast"); S_cb = sem("c_bcast"); S_dA = sem("dA_ready"); S_bm = sem("bx_made")
            S_sc = sem("scanned"); S_sv = sem("state_saved"); S_cm = sem("h_weighted"); S_ya = sem("y_added")
            S_yT = sem("y_transposed"); S_x1 = sem("x1_made")
            S_g = sem("gate_mm"); S_up = sem("up_mm"); S_th = sem("tanh_done"); S_hg = sem("half_gated")
            S_gt = sem("gated"); S_ah = sem("gated_hi"); S_al = sem("gated_lo")
            S_dm = sem("down_mm"); S_de = sem("down_added"); S_x2 = sem("x2_stored")
            S_fill = sem("slots_filled")

            first, second = range(HALF), range(HALF, M0)
            quanta = [(w, j) for h in (first, second) for q in (("gate", "up"), ("down",)) for j in h for w in q]
            sizes = [0, 0, 4, 4] + [3, 3, 2] * 4 + [3, 3, 2] + [0]
            ffn_slots = [quanta[sum(sizes[:i]):sum(sizes[:i + 1])] for i in range(len(sizes))]
            assert sum(sizes) == len(quanta)
            NSLOT = len(ffn_slots)
            serves = [("up", j) for j in range(HALF)] + [("down", k) for k in range(HALF)] + \
                     [("up", j) for j in range(HALF, M0)] + [("down", k) for k in range(HALF, M0)]
            LOADS = len(serves)
            per_chunk = [len(range(r, LOADS, RING)) for r in range(RING)]
            load_of = {w: s for s, w in enumerate(serves)}

            def ring_ready(pe, c, what):
                s = load_of[what]
                r = s % RING
                pe.wait_ge(S_ring[r], 16 * (per_chunk[r] * c + s // RING + 1))
                return ring[:, r, :]

            kinds = ["u", "u", "d"] * 4
            number_of = [kinds[:i].count(kinds[i]) for i in range(len(kinds))]
            prep_slots = {2: 0} | {4 + n: n + 1 for n in range(len(kinds) - 1)}

            with nc.Block() as block:
                @block.sync
                def _(sp):
                    def load_raw(kind, g):
                        if kind == "d":
                            src = a["wdT"].rearrange("(m p) h -> p m h", p=P)[:, :, P * g:P * g + P]
                            sp.dma_start(rawd.rearrange("p (m h) -> p m h", m=M0), src).then_inc(S_rawd, 16)
                        else:
                            src = a["wgT" if g < 4 else "wuT"].rearrange("(k p) i -> p k i", p=P)[:, :, 512 * (g % 4):512 * (g % 4) + 512]
                            sp.dma_start(raw[g % 2], src).then_inc(S_raw[g % 2], 16)

                    def store_prep(i):
                        g = number_of[i]
                        for m in range(4):
                            sp.wait_ge(S_pl, 4 * i + m + 1)
                            if kinds[i] == "u":
                                b = g % 4
                                dst = a["w_up"].rearrange("(b j) p k w c -> b w k p j c", b=4)[b, g // 4, m]
                                sp.dma_start(dst, stage_u[m].rearrange("p (j c) -> p j c", j=4).bitcast(fp32)).then_inc(S_su[m], 16)
                            else:
                                for part in range(2):
                                    dst = a["w_down"].rearrange("(x m) p s (g c) -> m s g p x c", x=4, g=4)[m, part, g]
                                    sp.dma_start(dst, stage_d[m % 2][part].rearrange("p (x c) -> p x c", x=4).bitcast(fp32)).then_inc(S_sd[m % 2], 16)

                    def fill_slots(e, n):
                        sp.dma_start(a["slots"][ds(e * P, n * P), :].rearrange("(e p) c -> p e c", p=P),
                                     a["empty"].unsqueeze(1).to_broadcast([P, n, ROW])).then_inc(S_fill, 16)

                    def zero_rows(c):
                        sp.dma_start(chunk(acc[1], c), a["empty"][:, 0:D].unsqueeze(1).to_broadcast([P, TT, D])).then_inc(S_fill, 16)

                    def load_ring(c, s, first=False):
                        r = s % RING
                        if not first:
                            kind, j = serves[s - RING if s >= RING else max(range(r, LOADS, RING))]
                            b = c if s >= RING else c - 1
                            if kind == "up":
                                sp.wait_ge(S_up, M0 * b + j + 1)
                            elif j % HALF == HALF - 1:
                                sp.wait_ge(S_dm, 8 * b + 4 * (j // HALF) + 4)
                            else:
                                sp.wait_ge(S_dk, 2 * (HALF - 1) * b + (HALF - 1) * (j // HALF) + j % HALF + 1)
                        kind, j = serves[s]
                        src = a["w_up"][j].rearrange("p k w c -> p (k w c)") if kind == "up" else a["w_down"][j].rearrange("p s h -> p (s h)")
                        sp.dma_start(ring[:, r, :].bitcast(fp32), src).then_inc(S_ring[r], 16)

                    sp.dma_start(xin[:, :, :], chunk(a["x"][0], 0)).then_inc(S_x, 16)
                    for dst, src in ((ident[:, :], a["ident"]), (wxp[:, :, 0:96], a["wxpT"].rearrange("(k p) e -> p k e", p=P)),
                                     (wxp[:, :, 96:P], a["wxpT"][:, 64:96].rearrange("(k p) e -> p k e", p=P)),
                                     (wdt[:, :], a["wdtT"]), (vec[:, :], a["vec"]),
                                     (an[:, :, :], a["A_log"].rearrange("(k p) n -> p k n", p=P)),
                                     (had[:, :, :], a["had"].rearrange("p (s q) -> p s q", s=2)),
                                     (self32[:, :], a["sel"]),
                                     (wsdp, a["ws_dp"].unsqueeze(0).to_broadcast([P, D]))):
                        sp.dma_start(dst, src).then_inc(S_w, 16)
                    load_raw("u", 0); load_raw("d", 0); load_raw("u", 1)
                    for v in acc:
                        sp.dma_start(v[T:NROWS, :], a["empty"][:, 0:D]).then_inc(S_fill, 16)
                    for i, kind in enumerate(kinds):
                        store_prep(i)
                        g = number_of[i] + (2 if kind == "u" else 1)
                        if g < kinds.count(kind):
                            sp.wait_ge(S_pmm, 4 * i + 4)
                            load_raw(kind, g)
                    for s in S_su:
                        sp.wait_ge(s, 16 * 8)
                    for s in S_sd:
                        sp.wait_ge(s, 16 * 16)
                    for s in range(RING):
                        load_ring(0, s, first=True)
                    fill_slots(0, E // 4)
                    zero_rows(0)
                    sp.wait_ge(S_x1, 4)
                    sp.dma_start(xin[:, :, :], chunk(a["x"][0], 1)).then_inc(S_x, 16)

                    def iteration(c, following):
                        for s in range(RING, LOADS):
                            load_ring(c - 1, s)
                            if s in (4, 7, 18, 21):
                                fill_slots(c * (E // 4) + 4 * (4, 7, 18, 21).index(s), 4)
                        zero_rows(c)
                        sp.wait_ge(S_de, 8 * c)
                        sp.dma_start(chunk(a["x2"], c - 1), x1[:, :, :]).then_inc(S_x2, 16)
                        for s in range(RING):
                            load_ring(c, s)
                        if following:
                            sp.wait_ge(S_x1, 4 * c + 4)
                            sp.dma_start(xin[:, :, :], chunk(a["x"][0], c + 1)).then_inc(S_x, 16)

                    with sp.Fori(1, NCH - 1) as c:
                        iteration(c, True)
                    iteration(NCH - 1, False)
                    for s in range(RING, LOADS):
                        load_ring(NCH - 1, s)
                    sp.wait_ge(S_de, 8 * NCH)
                    sp.dma_start(chunk(a["x2"], NCH - 1), x1[:, :, :]).then_inc(S_x2, 16)
                    sp.wait_ge(S_x2, 16 * NCH)
                    sp.wait_ge(S_fill, 16 * (2 + 1 + 4 * (NCH - 1) + NCH))

                @block.tensor
                def _(pe):
                    def transposes(n, c, t, b):
                        pe.wait_ge(n.xn, 4 * c + t + 1)
                        for k in range(KT):
                            last = nc.tensor.transpose(b[:, k * P:(k + 1) * P], xnt[:, t % 2, k * P:(k + 1) * P], ident[:, :])
                        last.then_inc(n.tp, 1)

                    def head(c, side):
                        wait(pe, S_bm, NS * c)
                        wait(pe, S_cm, NS * c)
                        wait(pe, n2.lo, 4 * c)
                        for t in range(TT):
                            transposes(n1, c, t, HB[t])
                        side(0)
                        pe.wait_ge(n1.xT, 4 * c + 4)
                        for k in range(KT):
                            last = nc.tensor.matmul(HB[0][:, :], wxp[:, k, :], y[:, k, :], start=(k == 0), stop=(k == KT - 1))
                        last.then_inc(S_xd, 1)
                        side(1)
                        pe.wait_ge(S_h2, c + 1)
                        for k in range(KT):
                            nc.tensor.matmul(HB[(k + 1) % 4][:, :], wdt[:, k * P:(k + 1) * P], dtr,
                                             start=True, stop=True).then_inc(S_dt, 1)
                        side(2)
                        side(3)
                        pe.wait_ge(S_rel, 4 * c + 4)

                    def bcast(c, n):
                        wait(pe, S_bm, NS * c + n - 1 if n >= 2 else 0)
                        nc.tensor.matmul(PB[n % 2][:, :], sel[:, n:n + 1].to_broadcast([P, P]), xdr[:, :],
                                         start=True, stop=True).then_inc(S_bb, 1)
                        wait(pe, S_cm, NS * c + n - 1 if n >= 2 else 0)
                        nc.tensor.matmul(PC[n % 2][:, :], sel[:, NS + n:NS + n + 1].to_broadcast([P, P]), xdr[:, :],
                                         start=True, stop=True).then_inc(S_cb, 1)

                    def states(c, side):
                        bcast(c, 0)
                        for n in range(NS):
                            if n + 1 < NS:
                                bcast(c, n + 1)
                            side(4 + n)

                    def tail(c):
                        wait(pe, S_de, 8 * c)
                        pe.wait_ge(S_ya, NS * (c + 1))
                        for t in range(TT):
                            for k in range(KT):
                                last = nc.tensor.transpose(PF[t][:, k * P:(k + 1) * P], y[:, k, t * P:(t + 1) * P], ident[:, :])
                            last.then_inc(S_yT, 1)
                        for t in range(TT):
                            transposes(n2, c, t, HB[t])

                    def ffn_step(c, kind, j):
                        if kind == "gate":
                            if j == 0:
                                pe.wait_ge(n2.lo, 4 * c + 4)
                            if j == HALF:
                                pe.wait_ge(S_de, 8 * c + 4)
                            if j % HALF >= 2:
                                pe.wait_ge(S_gt, M0 * c + j - 1)
                            ring_ready(pe, c, ("up", j))
                        if kind != "down":
                            lo = ring[:, load_of["up", j] % RING, :].rearrange("p (k w q) -> p k w q", k=KT, w=2)
                            which, s = (0, S_g) if kind == "gate" else (1, S_up)
                            b = PF[2 * (j % 2) + which]
                            w0 = which * F0 + j * P
                            for k in range(KT):
                                nc.tensor.matmul(b[:, :], wug[:, k, w0:w0 + P], xn2T[:, 0, k, :], start=(k == 0), stop=False)
                                nc.tensor.matmul(b[:, :], wug[:, k, w0:w0 + P], xn2T[:, 1, k, :], start=False, stop=False)
                                last = nc.tensor.matmul(b[:, :], lo[:, k, which, :], xn2T[:, 0, k, :], start=False, stop=(k == KT - 1))
                            last.then_inc(s, 1)
                        else:
                            half, k = j // HALF, j % HALF
                            if k == 0:
                                pe.wait_ge(S_gt, M0 * c + HALF * (half + 1))
                            pe.wait_ge(S_al, M0 * c + j + 1)
                            w = ring_ready(pe, c, (kind, j)).rearrange("p (s h) -> p s h", s=2)
                            for t in range(TT):
                                tok = slice(t * P, (t + 1) * P)
                                nc.tensor.matmul(PF[t][:, :], act8[:, 0, k, tok], w[:, 0, :], start=(k == 0), stop=False)
                                nc.tensor.matmul(PF[t][:, :], act8[:, 0, k, tok], w[:, 1, :], start=False, stop=False)
                                last = nc.tensor.matmul(PF[t][:, :], act8[:, 1, k, tok], w[:, 0, :], start=False, stop=(k == HALF - 1))
                                if k == HALF - 1:
                                    last.then_inc(S_dm, 1)
                            if k < HALF - 1:
                                last.then_inc(S_dk, 1)

                    def ffn(c):
                        return lambda slot: [ffn_step(c, *s) for s in ffn_slots[slot]]

                    def prep(slot):
                        if slot not in prep_slots:
                            return
                        i = prep_slots[slot]
                        g = number_of[i]
                        if kinds[i] == "u":
                            pe.wait_ge(S_raw[g % 2], 16 * (g // 2 + 1))
                        else:
                            pe.wait_ge(S_bf, 4 * g + 4)
                        for m in range(4):
                            wait(pe, S_pl, 4 * (i - 1) + m + 1 if i else 0)
                            for k in range(4):
                                x = raw[g % 2][:, k, :] if kinds[i] == "u" else \
                                    rawd.rearrange("p (x m h) -> p x m h", x=4, m=4)[:, :, k, :]
                                last = nc.tensor.matmul(PF[m][:, :], had[:, 0 if H4[m][k] > 0 else 1, :], x,
                                                        start=(k == 0), stop=(k == 3))
                            last.then_inc(S_pmm, 1)

                    pe.wait_ge(S_w, 16 * 9)
                    pe.wait_ge(S_sel, 1)
                    head(0, prep)
                    states(0, prep)
                    pe.wait_ge(S_pl, 4 * len(kinds))
                    tail(0)
                    with pe.Fori(1, NCH) as c:
                        f = ffn(c - 1)
                        head(c, f)
                        states(c, f)
                        tail(c)
                    for slot in range(NSLOT):
                        ffn(NCH - 1)(slot)

                @block.scalar
                def _(act):
                    def evac(n, c, t, b, dst):
                        act.wait_ge(n.tp, 4 * c + t + 1)
                        nc.scalar.activation(dst[:, :, t * P:(t + 1) * P], b[:, :].rearrange("p (k q) -> p k q", k=KT),
                                             ACT.Copy).then_inc(n.xT, 1)

                    def head(c, side):
                        for t in range(TT):
                            evac(n1, c, t, HB[t], y)
                        side(0)
                        act.wait_ge(S_xd, c + 1)
                        nc.scalar.activation(dtr, HB[0][0:R, :], ACT.Copy)
                        nc.scalar.activation(xdr[:, :], HB[0][:, :], ACT.Copy).then_inc(S_hi, 1)
                        side(1)
                        for k in range(KT):
                            act.wait_ge(S_dt, 4 * c + k + 1)
                            nc.scalar.activation(dl[:, k, :], HB[(k + 1) % 4][:, :], ACT.Abs, bias=b_dt[:, k:k + 1]).then_inc(S_abs, 1)
                        act.wait_ge(S_abs, 4 * c + 4)
                        nc.scalar.activation(dl[:, :, :], dl[:, :, :], ACT.Exp, scale=-1.0).then_inc(S_exp, 1)
                        side(2)
                        act.wait_ge(S_exp, c + 1)
                        nc.scalar.activation(u[:, :, :], dl[:, :, :], ACT.Ln, bias=1.0).then_inc(S_ln, 1)
                        side(3)
                        act.wait_ge(S_u, c + 1)
                        for k in range(KT):
                            last = nc.scalar.activation(y[:, k, :], y[:, k, :], ACT.Copy, scale=dpar[:, k:k + 1])
                        last.then_inc(S_yi, 1)

                    def decay(c, n):
                        wait(act, S_sc, NS * c + n - 1)
                        for k in range(KT):
                            last = nc.scalar.activation(dA[n % 2][:, k, :], dl[:, k, :], ACT.Exp, scale=an[:, k, n:n + 1])
                        last.then_inc(S_dA, 1)

                    def tail(c):
                        for t in range(TT):
                            evac(n2, c, t, HB[t], xn2T[:, 0, :, :])

                    def ffn_step(c, kind, j):
                        if kind == "up":
                            act.wait_ge(S_g, M0 * c + j + 1)
                            if j >= 2:
                                act.wait_ge(S_al, M0 * c + j - 1)
                            nc.scalar.activation(th[:, j % 2, :], PF[2 * (j % 2)][:, :], ACT.Tanh, scale=gsh[:, j:j + 1]).then_inc(S_th, 1)

                    def split_hi(c, kind, j):
                        if kind == "up":
                            act.wait_ge(S_gt, M0 * c + j + 1)
                            nc.scalar.activation(act8[:, 0, j % HALF, :], th[:, j % 2, :], ACT.Copy).then_inc(S_ah, 1)

                    def ffn(c):
                        def f(slot):
                            for step in (ffn_step, split_hi):
                                for s in ffn_slots[slot - 1] if slot >= 1 else ():
                                    step(c, *s)
                        return f

                    def prep(slot):
                        if slot - 1 not in prep_slots:
                            return
                        i = prep_slots[slot - 1]
                        g = number_of[i]
                        for m in range(4):
                            act.wait_ge(S_pmm, 4 * i + m + 1)
                            if kinds[i] == "u":
                                nc.scalar.activation(wug[:, m, 512 * g:512 * g + 512], PF[m][:, :], ACT.Copy,
                                                     scale=su_ug[:, m:m + 1]).then_inc(S_ph, 1)
                            else:
                                wait(act, S_sd[m % 2], 32 * (2 * g + m // 2))
                                nc.scalar.activation(stage_d[m % 2][0], PF[m][:, :], ACT.Copy).then_inc(S_ph, 1)

                    act.wait_ge(S_w, 16 * 9)
                    nc.scalar.activation(an[:, :, :], an[:, :, :], ACT.Exp).then_inc(S_an, 1)
                    nc.scalar.activation(sel[:, :], self32[:, :], ACT.Copy).then_inc(S_sel, 1)
                    head(0, prep)
                    act.wait_ge(S_an, 2)
                    act.wait_ge(S_dl, 1)
                    for n in range(NS):
                        decay(0, n)
                        prep(4 + n)
                    act.wait_ge(S_cs, 4)
                    tail(0)
                    with act.Fori(1, NCH) as c:
                        f = ffn(c - 1)
                        head(c, f)
                        act.wait_ge(S_dl, c + 1)
                        for n in range(NS):
                            decay(c, n)
                            f(4 + n)
                        f(NSLOT)
                        tail(c)
                    for slot in range(NSLOT + 1):
                        ffn(NCH - 1)(slot)

                @block.vector
                def _(dve):
                    def norm(n, c, src):
                        norm_stats(dve, n, c, src)
                        dve.wait_ge(n.rs, c + 1)
                        for t in range(TT):
                            if t >= 2:
                                dve.wait_ge(n.tp, 4 * c + t - 1)
                            normalize(n, t, xnt[:, t % 2, :], src)

                    def head(c, side):
                        dve.wait_ge(S_x, 16 * (c + 1))
                        wait(dve, n2.tp, 4 * c)
                        norm(n1, c, xin)
                        side(0)
                        dve.wait_ge(S_hi, c + 1)
                        nc.vector.tensor_tensor(xdr[96:P, :], HB[0][96:P, :], xdr[96:P, :].bitcast(fp32), ALU.subtract).then_inc(S_h2, 1)
                        side(1)
                        wait(dve, S_ya, NS * c)
                        for k in range(KT):
                            dve.wait_ge(S_abs, 4 * c + k + 1)
                            nc.vector.tensor_scalar(bx[0][:, k, :], HB[(k + 1) % 4][:, :], b_dt[:, k:k + 1], 0.0, ALU.add, ALU.max).then_inc(S_rel, 1)
                        side(2)
                        dve.wait_ge(S_exp, c + 1)
                        nc.vector.tensor_scalar(bx[1][:, :, :], dl[:, :, :], 1.0, 1.0, ALU.add, ALU.subtract).then_inc(S_sp, 1)
                        dve.wait_ge(S_sp, 3 * c + 1)
                        nc.vector.tensor_tensor(bx[1][:, :, :], dl[:, :, :], bx[1][:, :, :], ALU.subtract).then_inc(S_sp, 1)
                        dve.wait_ge(S_sp, 3 * c + 2)
                        nc.vector.tensor_tensor(bx[1][:, :, :], bx[1][:, :, :], bx[0][:, :, :], ALU.add).then_inc(S_sp, 1)
                        side(3)
                        dve.wait_ge(S_ln, c + 1)
                        dve.wait_ge(S_sp, 3 * c + 3)
                        nc.vector.tensor_tensor(dl[:, :, :], u[:, :, :], bx[1][:, :, :], ALU.add).then_inc(S_dl, 1)
                        dve.wait_ge(S_dl, c + 1)
                        nc.vector.tensor_tensor(u[:, :, :], dl[:, :, :], y[:, :, :], ALU.mult).then_inc(S_u, 1)

                    def scan(c, n, side):
                        b, i = bx[n % 2], NS * c + n
                        dve.wait_ge(S_bb, i + 1)
                        wait(dve, S_ya, i - 1)
                        if n == 0:
                            dve.wait_ge(S_u, c + 1)
                        nc.vector.tensor_tensor(b[:, :, :], u[:, :, :], PB[n % 2][:, :].unsqueeze(1).to_broadcast([P, KT, CH]),
                                                ALU.mult).then_inc(S_bm, 1)
                        side(4 + n)
                        dve.wait_ge(S_dA, i + 1)
                        dve.wait_ge(S_bm, i + 1)
                        for k in range(KT):
                            last = nc.vector.tensor_tensor_scan(b[:, k, :], dA[n % 2][:, k, :], b[:, k, :], state[:, k, n:n + 1],
                                                                ALU.mult, ALU.add)
                        last.then_inc(S_sc, 1)
                        dve.wait_ge(S_sc, i + 1)
                        nc.vector.tensor_copy(state[:, :, n:n + 1], b[:, :, CH - 1:CH]).then_inc(S_sv, 1)
                        dve.wait_ge(S_cb, i + 1)
                        dve.wait_ge(S_sv, i + 1)
                        nc.vector.tensor_tensor(b[:, :, :], b[:, :, :], PC[n % 2][:, :].unsqueeze(1).to_broadcast([P, KT, CH]),
                                                ALU.mult).then_inc(S_cm, 1)

                    def tail(c):
                        wait(dve, S_x2, 16 * c)
                        for t in range(TT):
                            dve.wait_ge(S_yT, 4 * c + t + 1)
                            nc.vector.tensor_tensor(x1[:, t, :], xin[:, t, :], PF[t][:, :], ALU.add).then_inc(S_x1, 1)
                        dve.wait_ge(S_x1, 4 * c + 4)
                        dve.wait_ge(n1.tp, 4 * c + 4)
                        norm(n2, c, x1)
                        for t in range(TT):
                            dve.wait_ge(n2.xT, 4 * c + t + 1)
                            tok = slice(t * P, (t + 1) * P)
                            nc.vector.tensor_tensor(xn2T[:, 1, :, tok], HB[t][:, :].rearrange("p (k q) -> p k q", k=KT),
                                                    xn2T[:, 0, :, tok].bitcast(fp32), ALU.subtract).then_inc(n2.lo, 1)

                    def ffn_step(c, kind, j):
                        if kind == "up":
                            g, up = PF[2 * (j % 2)], PF[2 * (j % 2) + 1]
                            dve.wait_ge(S_th, M0 * c + j + 1)
                            nc.vector.scalar_tensor_tensor(out=th[:, j % 2, :], in0=th[:, j % 2, :], scalar=1.0, in1=g[:, :],
                                                           op0=ALU.add, op1=ALU.mult).then_inc(S_hg, 1)
                            dve.wait_ge(S_up, M0 * c + j + 1)
                            dve.wait_ge(S_hg, M0 * c + j + 1)
                            nc.vector.scalar_tensor_tensor(out=th[:, j % 2, :], in0=up[:, :], scalar=cs[:, j:j + 1],
                                                           in1=th[:, j % 2, :], op0=ALU.mult, op1=ALU.mult).then_inc(S_gt, 1)
                        elif kind == "down" and j % HALF == HALF - 1:
                            half = j // HALF
                            for t in range(TT):
                                dve.wait_ge(S_dm, 8 * c + 4 * half + t + 1)
                                if half == 1:
                                    dve.wait_ge(S_de, 8 * c + t + 1)
                                nc.vector.tensor_tensor(x1[:, t, :], x1[:, t, :], PF[t][:, :], ALU.add).then_inc(S_de, 1)

                    def ffn(c):
                        return lambda slot: [ffn_step(c, *s) for s in (ffn_slots[slot - 1] if slot >= 1 else ())]

                    def prep(slot):
                        if slot - 1 not in prep_slots:
                            return
                        i = prep_slots[slot - 1]
                        g = number_of[i]
                        for m in range(4):
                            dve.wait_ge(S_ph, 4 * i + m + 1)
                            if kinds[i] == "u":
                                wait(dve, S_su[m], 16 * g)
                                nc.vector.scalar_tensor_tensor(out=stage_u[m], in0=PF[m][:, :], scalar=su_ug[:, m:m + 1],
                                                               in1=wug[:, m, 512 * g:512 * g + 512].bitcast(fp32),
                                                               op0=ALU.mult, op1=ALU.subtract).then_inc(S_pl, 1)
                            else:
                                wait(dve, S_sd[m % 2], 32 * (2 * g + m // 2))
                                nc.vector.tensor_tensor(stage_d[m % 2][1], PF[m][:, :], stage_d[m % 2][0].bitcast(fp32),
                                                        ALU.subtract).then_inc(S_pl, 1)

                    nc.vector.memset(state[:, :, :], 0.0).then_inc(S_st0, 1)
                    nc.vector.memset(eps[:, :], EPS)
                    nc.vector.memset(neghalf[:, :], -0.5).then_inc(S_const, 1)
                    dve.wait_ge(S_w, 16 * 9)
                    dve.wait_ge(S_an, 1)
                    nc.vector.tensor_scalar(an[:, :, :], an[:, :, :], -1.0, None, ALU.mult).then_inc(S_an, 1)
                    nc.vector.tensor_scalar(gsh[:, :], wsg, 0.5 / D ** 0.5, None, ALU.mult).then_inc(S_cs, 1)
                    nc.vector.tensor_tensor(cs[:, :], wsg, wsu, ALU.mult).then_inc(S_cs, 1)
                    dve.wait_ge(S_cs, 2)
                    nc.vector.tensor_tensor(cs[:, :], cs[:, :], su_dp, ALU.mult).then_inc(S_cs, 1)
                    dve.wait_ge(S_cs, 3)
                    nc.vector.tensor_scalar(cs[:, :], cs[:, :], 0.5 / (D * F0 ** 0.5), None, ALU.mult).then_inc(S_cs, 1)
                    dve.wait_ge(S_st0, 1)
                    head(0, prep)
                    for n in range(NS):
                        scan(0, n, prep)
                    tail(0)
                    with dve.Fori(1, NCH) as c:
                        f = ffn(c - 1)
                        head(c, f)
                        for n in range(NS):
                            scan(c, n, f)
                        f(NSLOT)
                        tail(c)
                    for slot in range(NSLOT + 1):
                        ffn(NCH - 1)(slot)

                @block.gpsimd
                def _(pool):
                    def add(c, n):
                        i = NS * c + n
                        pool.wait_ge(S_cm, i + 1)
                        wait(pool, S_ya, i)
                        if n == 0:
                            pool.wait_ge(S_yi, c + 1)
                        nc.gpsimd.tensor_tensor(y[:, :, :], y[:, :, :], bx[n % 2][:, :, :], ALU.add).then_inc(S_ya, 1)

                    def split_lo(c, slot):
                        for kind, j in ffn_slots[slot - 1] if slot >= 1 else ():
                            if kind == "up":
                                pool.wait_ge(S_const, 1)
                                pool.wait_ge(S_ah, M0 * c + j + 1)
                                nc.gpsimd.tensor_tensor(act8[:, 1, j % HALF, :], th[:, j % 2, :], act8[:, 0, j % HALF, :].bitcast(fp32),
                                                        ALU.subtract).then_inc(S_al, 1)

                    def butterfly(g, part):
                        p, q = (rawd, sums) if part == 1 else (sums, rawd)
                        if part == 0:
                            pool.wait_ge(S_rawd, 16 * (g + 1))
                            v = rawd.rearrange("p (m h) -> p m h", m=M0)
                            nc.gpsimd.tensor_tensor(v, v, wsdp[:, g * P:(g + 1) * P].unsqueeze(1).to_broadcast([P, M0, P]), ALU.mult).then_inc(S_wsc, 1)
                            return
                        if part == 1:
                            pool.wait_ge(S_wsc, g + 1)
                            pool.wait_ge(S_bf, 4 * g) if g else None
                        else:
                            pool.wait_ge(S_bf, 4 * g + 2)
                        shape = "p (a b c) -> p a b c" if part == 1 else "p (b a c) -> p a b c"
                        pv, qv = (v.rearrange(shape, a=2, b=2) for v in (p, q))
                        for i, op in enumerate((ALU.add, ALU.subtract)):
                            nc.gpsimd.tensor_tensor(qv[:, :, i, :], pv[:, :, 0, :], pv[:, :, 1, :], op).then_inc(S_bf, 1)

                    pool.wait_ge(S_w, 16 * 9)
                    norm_rstd(pool, n1, 0)
                    for part in range(3):
                        butterfly(0, part)
                    for n in range(NS):
                        add(0, n)
                        for part in {2: (0,), 0: (1, 2), 1: ()}[n % 3] if 2 <= n < 10 else ():
                            butterfly((n + 1) // 3, part)
                    norm_rstd(pool, n2, 0)
                    with pool.Fori(1, NCH) as c:
                        norm_rstd(pool, n1, c)
                        for slot in range(4):
                            split_lo(c - 1, slot)
                        for n in range(NS):
                            split_lo(c - 1, 4 + n)
                            add(c, n)
                        split_lo(c - 1, NSLOT)
                        norm_rstd(pool, n2, c)
                    for slot in range(NSLOT + 1):
                        split_lo(NCH - 1, slot)

        B = ExitStack()
        with B:
            wx = sb(B, "wx", [P, 2, KT, I1], f32r)
            wz = sb(B, "wz", [P, 2, KT, I1], f32r)
            wo = sb(B, "wo", [P, 2, M1, D], f32r)
            gate = sb(B, "gate", [P, KT, E])
            dh = sb(B, "dh", [P, M1])
            before_f = sb(B, "before_f", [P, P])
            before = sb(B, "before", [P, P], bf16)
            ones = sb(B, "ones", [P, P], bf16)
            chosen_sum = sb(B, "chosen_sum", [P, E], bf16)
            first_slot = sb(B, "first_slot", [P, E])
            number = sb(B, "number", [P, 1])
            xb = sb(B, "xb", [P, TT, D])
            xr = sb(B, "xr", [P, TT, D])
            x3 = sb(B, "x3", [P, TT, D])
            xn3 = sb(B, "xn3", [P, 2, D])
            xT = sb(B, "xT", [P, 2, KT, CH], f32r)
            gm = sb(B, "gm", [P, 2, M1, CH], f32r)
            tz = sb(B, "tz", [P, 2, CH])
            row = sb(B, "row", [P, 2, ROW])
            x4T = sb(B, "x4T", [P, KT, P])
            rt = sb(B, "rt", [P, 8, E])
            rc = sb(B, "rc", [P, 8])
            top8 = sb(B, "top8", [P, 3, TOPK])
            chosen_b = sb(B, "chosen_b", [P, E], bf16)
            idx = sb(B, "idx", [P, 2, TOPK], u32)
            fold_rows = sb(B, "fold_rows", [P, TT, D])
            spare = sb(B, "spare", [P, 2, 4, 512])
            BZ, BX, BT, BO = bank[0:2], bank[2:4], bank[4:6], bank[6:8]
            out_bank = lambda c, t: (BO if c < NCH - 1 else BZ)[t % 2]

            n3, n4 = Norm("n3"), Norm("n4")
            S_w = [sem("w_in_x0"), sem("w_in_x1")]; S_pl = sem("b_plain"); S_big = [sem("b_big0"), sem("b_big1")]; S_sm = sem("b_small")
            S_fm = sem("fold_mm"); S_fh = sem("fold_hi"); S_fl = sem("fold_lo"); S_wh = sem("weight_hi"); S_wl = sem("weight_lo")
            S_xb = sem("xb_in"); S_xr = sem("xr_in"); S_zm = sem("z_mm"); S_xm = sem("xc_mm"); S_tz = sem("z_tanh")
            S_zg = sem("z_gated"); S_gf = sem("g_made"); S_gh = sem("g_hi"); S_gl = sem("g_lo")
            S_om = sem("out_mm"); S_x3 = sem("x3_made"); S_st = sem("x3_stored")
            S_lg = sem("logits_mm"); S_r = sem("route_step"); S_ex = sem("route_exp"); S_pm = sem("place_mm")
            S_sct = [sem("rows_out0"), sem("rows_out1")]
            RS = 17

            S_bt = sem("triangle_ready")

            stage, fold_in, stage_p = [xr[:, :, :], spare[:, 0]], [x3[:, :, :], fold_rows[:, :, :]], spare[:, 1]
            conv, winz, wout = (a[n].rearrange("(k p) i -> p k i", p=P) for n in ("convT", "winzT", "woT"))
            conv_pieces = [conv[:, 4 * q:4 * q + 4, h * 512:h * 512 + 512] for h in range(2) for q in range(2)]
            pieces = [winz[:, :, h * 512:h * 512 + 512] for h in range(2)] + [wout[:, 4 * q:4 * q + 4, :] for q in range(2)]

            def plain(part, i):
                return wz[:, part, :, i * 512:i * 512 + 512] if i < 2 else wo[:, part, 4 * i - 8:4 * i - 4, :]

            with nc.Block() as block:

                @block.sync
                def _(sp):
                    def load(c):
                        sp.dma_start(xb[:, :, :], chunk(a["x2"], c)).then_inc(S_xb, 16)

                    def load_conv(i):
                        if i >= 2:
                            sp.wait_ge(S_fm, KT * (i - 1))
                        sp.dma_start(stage[i % 2], conv_pieces[i]).then_inc(S_big[i % 2], 16)

                    def load_plain(i):
                        wait(sp, S_wl, i)
                        sp.dma_start(stage_p, pieces[i]).then_inc(S_pl, 16)

                    for q in range(2):
                        sp.dma_start(fold_in[q], a["winx"].rearrange("(k p) h -> p k h", p=P)[:, 4 * q:4 * q + 4, :]).then_inc(S_w[q], 16)
                        load_conv(q)
                    for dst, src in ((gate[:, :, :], a["gateT"].rearrange("(k p) e -> p k e", p=P)), (dh[:, :], a["d1"]),
                                     (before_f[:, :], a["before"]), (first_slot[:, :], a["first_slot"]), (number[:, :], a["number"])):
                        sp.dma_start(dst, src).then_inc(S_sm, 16)
                    load(0)
                    load_plain(0)
                    load_plain(1)
                    load_conv(2)
                    load_plain(2)
                    load_conv(3)
                    load_plain(3)
                    sp.wait_ge(S_fm, 3 * KT)
                    sp.dma_start(xr[:, :, :], chunk(a["x2"], 0)).then_inc(S_xr, 16)
                    sp.wait_ge(n3.xn, 4)
                    load(1)
                    for c in range(NCH):
                        sp.wait_ge(S_x3, 4 * c + 4)
                        sp.dma_start(chunk(acc[0], c), x3[:, :, :]).then_inc(S_st, 16)
                        if c + 1 < NCH:
                            sp.dma_start(xr[:, :, :], chunk(a["x2"], c + 1)).then_inc(S_xr, 16)
                        if c + 2 < NCH:
                            sp.wait_ge(n3.xn, 4 * c + 8)
                            load(c + 2)
                    sp.wait_ge(S_st, 16 * NCH)

                def split3(out, w_of, x_of, n):
                    for k in range(n):
                        for wp, xp in ((0, 0), (1, 0), (0, 1)):
                            last = nc.tensor.matmul(out, w_of(wp, k), x_of(xp, k), start=(k == 0 and wp == 0 and xp == 0),
                                                    stop=(k == n - 1 and xp == 1))
                    return last

                @block.tensor
                def _(pe):
                    def norm_T(n, c, t, src):
                        pe.wait_ge(n.xn, 4 * c + t + 1)
                        for k in range(KT):
                            last = nc.tensor.transpose(BT[t % 2][:, k * P:(k + 1) * P], src(t)[:, k * P:(k + 1) * P], ident[:, :])
                        last.then_inc(n.tp, 1)

                    def norm3(c, t):
                        if t >= 2:
                            pe.wait_ge(n3.lo, 4 * c + t - 1)
                        norm_T(n3, c, t, lambda t: xn3[:, t % 2, :])

                    def mixer(c, m):
                        if m == 0:
                            pe.wait_ge(n3.lo, 4 * c + 4)
                        if m >= 2:
                            pe.wait_ge(S_gf, M1 * c + m - 1)
                        for b, w, s in ((BZ[m % 2], wz, S_zm), (BX[m % 2], wx, S_xm)):
                            split3(b[:, :], lambda q, k: w[:, q, k, m * P:(m + 1) * P], lambda q, k: xT[:, q, k, :], KT).then_inc(s, 1)

                    def out(c, t):
                        if t == 0:
                            pe.wait_ge(S_gl, M1 * (c + 1))
                        if t >= 2:
                            pe.wait_ge(S_x3, 4 * c + t - 1)
                        split3(out_bank(c, t)[:, :], lambda q, k: gm[:, q, k, t * P:(t + 1) * P],
                               lambda q, k: wo[:, q, k, :], M1).then_inc(S_om, 1)

                    def route_T(c, t):
                        norm_T(n4, c, t, lambda t: row[:, t % 2, 0:D])

                    def logits(c, t):
                        pe.wait_ge(n4.xT, 4 * c + t + 1)
                        for k in range(KT):
                            last = nc.tensor.matmul(BO[0][:, 0:E], x4T[:, k, :], gate[:, k, :], start=(k == 0), stop=(k == KT - 1))
                        last.then_inc(S_lg, 1)

                    def place(c, t):
                        pe.wait_ge(S_r, RS * (4 * c + t) + 10)
                        nc.tensor.matmul(BO[1][:, 0:E], before[:, :], chosen_b[:, :], start=True, stop=False)
                        nc.tensor.matmul(BO[1][:, 0:E], ones[:, :], chosen_sum[:, :], start=False, stop=True).then_inc(S_pm, 1)

                    def fold(half):
                        for q in range(2):
                            i = 2 * half + q
                            pe.wait_ge(S_w[q], 16)
                            pe.wait_ge(S_big[i % 2], 16 * (i // 2 + 1))
                            if q == 0 and half == 1:
                                pe.wait_ge(S_fl, KT)
                            for m in range(KT):
                                for k in range(4):
                                    last = nc.tensor.matmul(bank[m][:, :], fold_in[q][:, k, m * P:(m + 1) * P], stage[i % 2][:, k, :],
                                                            start=(k == 0 and q == 0), stop=(k == 3 and q == 1))
                                last.then_inc(S_fm, 1)
                    fold(0)
                    for t in range(TT):
                        norm3(0, t)
                    fold(1)
                    pe.wait_ge(S_fl, 2 * KT)
                    pe.wait_ge(S_wl, 4)

                    def body(c, routing, following):
                        for m in range(M1):
                            mixer(c, m)
                            if routing and m % 2 == 0:
                                route_T(c - 1, m // 2)
                                if m:
                                    place(c - 1, m // 2 - 1)
                            if routing and m % 2 == 1:
                                logits(c - 1, m // 2)
                        if routing:
                            place(c - 1, TT - 1)
                            pe.wait_ge(S_r, RS * 4 * c)
                        if following:
                            for t in range(TT):
                                out(c, t)
                                norm3(c + 1, t)
                            return
                        for step, t in ((out, 0), (out, 1), (route_T, 0), (out, 2), (logits, 0), (route_T, 1), (place, 0), (out, 3),
                                        (logits, 1), (place, 1), (route_T, 2), (logits, 2), (place, 2),
                                        (route_T, 3), (logits, 3), (place, 3)):
                            step(c, t)

                    for c in range(NCH):
                        body(c, c > 0, c + 1 < NCH)

                @block.scalar
                def _(act):
                    def split_hi(c, t):
                        act.wait_ge(n3.tp, 4 * c + t + 1)
                        nc.scalar.activation(xT[:, 0, :, t * P:(t + 1) * P], BT[t % 2][:, :].rearrange("p (k q) -> p k q", k=KT),
                                             ACT.Copy).then_inc(n3.xT, 1)

                    def mixer(c, m):
                        act.wait_ge(S_zm, M1 * c + m + 1)
                        if m >= 2:
                            act.wait_ge(S_gl, M1 * c + m - 1)
                        else:
                            wait(act, S_gl, M1 * c)
                        nc.scalar.activation(tz[:, m % 2, :], BZ[m % 2][:, :], ACT.Tanh, scale=0.5).then_inc(S_tz, 1)

                    def g_hi(c, m):
                        act.wait_ge(S_gf, M1 * c + m + 1)
                        nc.scalar.activation(gm[:, 0, m, :], tz[:, m % 2, :], ACT.Copy).then_inc(S_gh, 1)

                    def route_T(c, t):
                        act.wait_ge(n4.tp, 4 * c + t + 1)
                        nc.scalar.activation(x4T[:, :, :], BT[t % 2][:, :].rearrange("p (k q) -> p k q", k=KT), ACT.Copy).then_inc(n4.xT, 1)

                    def route_exp(c, t):
                        act.wait_ge(S_r, RS * (4 * c + t) + 2)
                        nc.scalar.activation(rt[:, 0, :], BO[0][:, 0:E], ACT.Exp, bias=rc[:, 1:2], accum_out=rc[:, 2:3]).then_inc(S_ex, 1)

                    def fold_hi(half):
                        for m in range(KT):
                            act.wait_ge(S_fm, KT * (2 * half + 1) + m + 1)
                            nc.scalar.activation(wx[:, 0, m, half * 512:half * 512 + 512], bank[m][:, :], ACT.Copy).then_inc(S_fh, 1)

                    def plain_hi(i):
                        act.wait_ge(S_pl, 16 * (i + 1))
                        nc.scalar.activation(plain(0, i), stage_p, ACT.Copy).then_inc(S_wh, 1)

                    plain_hi(0)
                    plain_hi(1)
                    fold_hi(0)
                    for t in range(TT):
                        split_hi(0, t)
                    plain_hi(2)
                    plain_hi(3)
                    fold_hi(1)

                    def body(c, routing, following):
                        for m in range(M1):
                            mixer(c, m)
                            g_hi(c, m)
                            if routing:
                                (route_exp if m % 2 else route_T)(c - 1, m // 2)
                        if following:
                            for t in range(TT):
                                split_hi(c + 1, t)

                    for c in range(NCH):
                        body(c, c > 0, c + 1 < NCH)
                    for t in range(TT):
                        route_T(NCH - 1, t)
                        route_exp(NCH - 1, t)

                @block.vector
                def _(dve):
                    def norm3(c):
                        dve.wait_ge(S_xb, 16 * (c + 1))
                        norm_stats(dve, n3, c, xb)
                        dve.wait_ge(n3.rs, c + 1)

                    def norm3_tile(c, t):
                        if t >= 2:
                            dve.wait_ge(n3.tp, 4 * c + t - 1)
                        normalize(n3, t, xn3[:, t % 2, :], xb)

                    def split_lo(c, t):
                        dve.wait_ge(n3.xT, 4 * c + t + 1)
                        hi = xT[:, 0, :, t * P:(t + 1) * P]
                        nc.vector.tensor_tensor(xT[:, 1, :, t * P:(t + 1) * P], BT[t % 2][:, :].rearrange("p (k q) -> p k q", k=KT),
                                                hi.bitcast(fp32), ALU.subtract).then_inc(n3.lo, 1)

                    def mixer(c, m):
                        dve.wait_ge(S_tz, M1 * c + m + 1)
                        nc.vector.scalar_tensor_tensor(out=tz[:, m % 2, :], in0=tz[:, m % 2, :], scalar=1.0, in1=BZ[m % 2][:, :],
                                                       op0=ALU.add, op1=ALU.mult).then_inc(S_zg, 1)
                        dve.wait_ge(S_xm, M1 * c + m + 1)
                        dve.wait_ge(S_zg, M1 * c + m + 1)
                        nc.vector.scalar_tensor_tensor(out=tz[:, m % 2, :], in0=BX[m % 2][:, :], scalar=dh[:, m:m + 1],
                                                       in1=tz[:, m % 2, :], op0=ALU.mult, op1=ALU.mult).then_inc(S_gf, 1)
                        dve.wait_ge(S_gh, M1 * c + m + 1)
                        nc.vector.tensor_tensor(gm[:, 1, m, :], tz[:, m % 2, :], gm[:, 0, m, :].bitcast(fp32), ALU.subtract).then_inc(S_gl, 1)

                    def out(c, t):
                        dve.wait_ge(S_om, 4 * c + t + 1)
                        if t == 0:
                            dve.wait_ge(S_xr, 16 * (c + 1))
                            wait(dve, S_st, 16 * c)
                        nc.vector.tensor_tensor(x3[:, t, :], xr[:, t, :], out_bank(c, t)[:, :], ALU.add).then_inc(S_x3, 1)

                    def norm4(c):
                        dve.wait_ge(S_x3, 4 * c + 4)
                        norm_stats(dve, n4, c, x3)
                        dve.wait_ge(n4.rs, c + 1)

                    def norm4_tile(t):
                        dve.wait_ge(S_x3, 4 * (NCH - 1) + t + 1)
                        nc.vector.bn_stats(st6[:, t, :], x3[:, t, :]).then_inc(n4.bn, 1)
                        dve.wait_ge(S_const, 1)
                        dve.wait_ge(n4.bn, NCH + t)
                        nc.vector.bn_aggr(mv[:, t, :], st6[:, t, :]).then_inc(n4.mv, 1)

                    def route(c, t, part):
                        i = 4 * c + t
                        r = row[:, t % 2, :]
                        pr, rest, chosen, key, v = (rt[:, j, :] for j in range(1, 6))

                        def after(s):
                            dve.wait_ge(S_const, 1)
                            dve.wait_ge(S_r, RS * i + s)

                        if part == 0:
                            wait(dve, S_sct[t % 2], 16 * TOPK * (2 * c + t // 2))
                            normalize(n4, t, r[:, 0:D], x3)
                        elif part == 1:
                            nc.vector.tensor_copy(r[:, ROW - 1:ROW], number[:, :])
                            dve.wait_ge(S_lg, i + 1)
                            nc.vector.reduce_max(rc[:, 0:1], BO[0][:, 0:E], AX.X).then_inc(S_r, 1)
                            after(1)
                            nc.vector.tensor_scalar(rc[:, 1:2], rc[:, 0:1], -1.0, None, ALU.mult).then_inc(S_r, 1)
                            after(2)
                            nc.vector.tensor_scalar(number[:, :], number[:, :], float(P), None, ALU.add).then_inc(S_r, 1)
                            dve.wait_ge(S_ex, i + 1)
                            nc.vector.reciprocal(rc[:, 3:4], rc[:, 2:3]).then_inc(S_r, 1)
                            after(4)
                            nc.vector.tensor_scalar(pr, rt[:, 0, :], rc[:, 3:4], None, ALU.mult).then_inc(S_r, 1)
                            after(5)
                            nc.vector.max(top8[:, 0, :], pr).then_inc(S_r, 1)
                            after(6)
                            nc.vector.match_replace(rest, top8[:, 0, :], pr, -1.0).then_inc(S_r, 1)
                            after(7)
                            nc.vector.tensor_scalar(chosen, rest, 0.0, None, ALU.is_lt).then_inc(S_r, 1)
                            nc.vector.reduce_sum(rc[:, 4:5], top8[:, 0, :], AX.X).then_inc(S_r, 1)
                            after(8)
                            nc.vector.tensor_copy(chosen_b[:, :], chosen).then_inc(S_r, 1)
                            after(9)
                            nc.vector.reciprocal(rc[:, 5:6], rc[:, 4:5]).then_inc(S_r, 1)
                        else:
                            after(11)
                            nc.vector.scalar_tensor_tensor(out=r[:, D:D + E], in0=pr, scalar=rc[:, 5:6], in1=chosen,
                                                           op0=ALU.mult, op1=ALU.mult).then_inc(S_r, 1)
                            dve.wait_ge(S_pm, i + 1)
                            nc.vector.tensor_tensor(chosen_sum[:, :], chosen_sum[:, :], chosen_b[:, :], ALU.add)
                            nc.vector.tensor_tensor(key, BO[1][:, 0:E], first_slot[:, :], ALU.add)
                            nc.vector.scalar_tensor_tensor(out=v, in0=BO[1][:, 0:E], scalar=float(CAP), in1=chosen,
                                                           op0=ALU.is_lt, op1=ALU.mult).then_inc(S_r, 1)
                            after(13)
                            nc.vector.tensor_tensor(key, key, v, ALU.mult).then_inc(S_r, 1)
                            after(14)
                            nc.vector.max(top8[:, 1, :], key).then_inc(S_r, 1)
                            after(15)
                            nc.vector.tensor_scalar(top8[:, 2, :], top8[:, 1, :], 0.0, FAR, ALU.is_equal, ALU.mult).then_inc(S_r, 1)
                            after(16)
                            nc.vector.scalar_tensor_tensor(out=idx[:, t % 2, :], in0=top8[:, 1, :], scalar=-1.0, in1=top8[:, 2, :],
                                                           op0=ALU.add, op1=ALU.add).then_inc(S_r, 1)

                    dve.wait_ge(S_sm, 80)
                    nc.vector.memset(ones[:, :], 1.0)
                    nc.vector.memset(chosen_sum[:, :], 0.0)
                    nc.vector.tensor_scalar(dh[:, :], dh[:, :], 0.5, None, ALU.mult)
                    nc.vector.tensor_copy(before[:, :], before_f[:, :]).then_inc(S_bt, 1)
                    def fold_lo(half):
                        for m in range(KT):
                            dve.wait_ge(S_fh, KT * half + m + 1)
                            cols = slice(half * 512, half * 512 + 512)
                            last = nc.vector.tensor_tensor(wx[:, 1, m, cols], bank[m][:, :], wx[:, 0, m, cols].bitcast(fp32), ALU.subtract)
                            last.then_inc(S_fl, 1)

                    def plain_lo(i):
                        dve.wait_ge(S_wh, i + 1)
                        nc.vector.tensor_tensor(plain(1, i), stage_p, plain(0, i).bitcast(fp32), ALU.subtract).then_inc(S_wl, 1)

                    norm3(0)
                    norm3_tile(0, 0)
                    norm3_tile(0, 1)
                    plain_lo(0)
                    plain_lo(1)
                    fold_lo(0)
                    for t in range(TT):
                        if t >= 2:
                            norm3_tile(0, t)
                        if t >= 1:
                            split_lo(0, t - 1)
                    split_lo(0, TT - 1)
                    plain_lo(2)
                    plain_lo(3)
                    fold_lo(1)

                    def body(c, routing, following):
                        if routing:
                            norm4(c - 1)
                        for m in range(M1):
                            if routing and m % 2 == 0:
                                route(c - 1, m // 2, 0)
                            mixer(c, m)
                            if routing and m % 2 == 1:
                                route(c - 1, m // 2, 1)
                            if routing and m % 2 == 0 and m:
                                route(c - 1, m // 2 - 1, 2)
                        if routing:
                            route(c - 1, TT - 1, 2)
                        if following:
                            norm3(c + 1)
                            for t in range(TT):
                                out(c, t)
                                norm3_tile(c + 1, t)
                                if t >= 1:
                                    split_lo(c + 1, t - 1)
                            split_lo(c + 1, TT - 1)
                            return
                        for step, t in (("out", 0), ("out", 1), (0, 0), ("out", 2), (0, 1), (1, 0), (2, 0), ("out", 3), (1, 1), (2, 1),
                                        (0, 2), (1, 2), (2, 2), (0, 3), (1, 3), (2, 3)):
                            if step == "out":
                                out(c, t)
                                norm4_tile(t)
                            else:
                                if step == 0:
                                    dve.wait_ge(n4.rs, NCH + t)
                                route(c, t, step)

                    for c in range(NCH):
                        body(c, c > 0, c + 1 < NCH)

                @block.gpsimd
                def _(pool):
                    def rows_out(c, t):
                        pool.wait_ge(S_const, 1)
                        pool.wait_ge(S_r, RS * (4 * c + t + 1))
                        for k in range(TOPK):
                            nc.gpsimd.indirect_dma_start(a["slots"][:, :], bass.IndirectOffsetOnAxis(idx[:, t % 2, k:k + 1], 0),
                                                         row[:, t % 2, :], None, bounds_check=E * P - 1, oob_is_err=False).then_inc(S_sct[t % 2], 16)

                    norm_rstd(pool, n3, 0)
                    def norm4_rstd(t):
                        pool.wait_ge(S_const, 1)
                        pool.wait_ge(n4.mv, NCH + t)
                        nc.gpsimd.tensor_tensor(ve[:, t:t + 1], mv[:, t, 1:2], eps[:, t:t + 1], ALU.add).then_inc(n4.ve, 1)
                        pool.wait_ge(n4.ve, NCH + t)
                        nc.gpsimd.tensor_tensor(rs[:, t:t + 1], ve[:, t:t + 1], neghalf[:, t:t + 1], ALU.pow).then_inc(n4.rs, 1)

                    for c in range(NCH + 1):
                        if c >= 1:
                            if c < NCH:
                                norm_rstd(pool, n4, c - 1)
                                for t in range(TT):
                                    rows_out(c - 1, t)
                            else:
                                for t in range(TT - 1):
                                    norm4_rstd(t)
                                rows_out(c - 1, 0)
                                norm4_rstd(TT - 1)
                                for t in range(1, TT):
                                    rows_out(c - 1, t)
                        if c + 1 < NCH:
                            norm_rstd(pool, n3, c + 1)
                    for s in S_sct:
                        pool.wait_ge(s, 16 * TOPK * 2 * NCH)

        C = ExitStack()
        with C:
            xe = sb(C, "xe", [P, SLOTS, ROW])
            wgu = sb(C, "wgu", [P, SLOTS, KT, 2 * FE])
            wde = sb(C, "wde", [FH, SLOTS, 2, D])
            xeT = sb(C, "xeT", [P, 2, KT, P])
            te = sb(C, "te", [P, 2, FE])
            he = sb(C, "he", [P, 2, FE])
            hT = sb(C, "hT", [FH, 2, 2, P])
            ye = sb(C, "ye", [P, SLOTS, D])
            wsc = sb(C, "wsc", [P, SLOTS])
            tok = sb(C, "tok", [P, SLOTS], u32)
            CX, CG, CHT, CO = bank[0:2], bank[2:4], bank[4:6], bank[6:8]
            S_xe = [sem(f"rows_in{i}") for i in range(SLOTS)]
            S_gu = [sem(f"gate_up_in{i}") for i in range(SLOTS)]
            S_dn = [sem(f"down_in{i}") for i in range(SLOTS)]
            S_xt = sem("rows_transposed"); S_xc = sem("rows_copied"); S_gm = sem("gate_up_mm"); S_et = sem("e_tanh")
            S_eg = sem("e_half_gated"); S_h = sem("h_made"); S_ht = sem("h_transposed"); S_hc = sem("h_copied")
            S_y = sem("down_e_mm"); S_ws = sem("slot_weights"); S_ys = sem("rows_scaled"); S_add = [sem("added0"), sem("added1")]

            with nc.Block() as block:
                def previous(q, i):
                    return (q, i - 1) if i else (q - 1, SLOTS - 1)

                def following(q, i):
                    return (q, i + 1) if i + 1 < SLOTS else (q + 1, 0)

                def steps(eng, f):
                    for i in range(SLOTS):
                        f(0, i, first=(i == 0))
                    with eng.Fori(1, E // SLOTS - 1) as q:
                        for i in range(SLOTS):
                            f(q, i)
                    for i in range(SLOTS):
                        f(E // SLOTS - 1, i, last=(i == SLOTS - 1))

                def rounds(eng, f):
                    for i in range(SLOTS):
                        f(0, i)
                    with eng.Fori(1, E // SLOTS) as q:
                        for i in range(SLOTS):
                            f(q, i)

                @block.sync
                def _(sp):
                    def load(q, i):
                        e = SLOTS * q + i
                        first = isinstance(q, int) and q == 0
                        if not first:
                            sp.wait_ge(S_ws, e - SLOTS + 1)
                            sp.wait_ge(S_gm, e - SLOTS + 1)
                        sp.dma_start(xe[:, i, :], a["slots"][ds(e * P, P), :]).then_inc(S_xe[i], 16)
                        for w, off in ((a["wg"], 0), (a["wu"], FE)):
                            sp.dma_start(wgu[:, i, :, off:off + FE], w.rearrange("e h f -> (e h) f")[ds(e * D, D), :]
                                         .rearrange("(k p) f -> p k f", p=P)).then_inc(S_gu[i], 16)
                        if not first:
                            sp.wait_ge(S_y, e - SLOTS + 1)
                        sp.dma_start(wde[:, i, :, :], a["wd"].rearrange("e f h -> (e f) h")[ds(e * FE, FE), :]
                                     .rearrange("(s p) h -> p s h", p=FH)).then_inc(S_dn[i], 16)
                    rounds(sp, load)

                @block.tensor
                def _(pe):
                    def rows_T(q, i):
                        e = SLOTS * q + i
                        pe.wait_ge(S_xe[i], 16 * (q + 1))
                        wait(pe, S_xc, e - 1)
                        for k in range(KT):
                            last = nc.tensor.transpose(CX[i % 2][:, k * P:(k + 1) * P], xe[:, i, k * P:(k + 1) * P], ident[:, :])
                        last.then_inc(S_xt, 1)

                    def gate_up(q, i):
                        e = SLOTS * q + i
                        pe.wait_ge(S_gu[i], 32 * (q + 1))
                        pe.wait_ge(S_xc, e + 1)
                        wait(pe, S_h, e - 1)
                        for k in range(KT):
                            last = nc.tensor.matmul(CG[i % 2][:, 0:2 * FE], xeT[:, i % 2, k, :], wgu[:, i, k, :],
                                                    start=(k == 0), stop=(k == KT - 1))
                        last.then_inc(S_gm, 1)

                    def h_T(q, i):
                        e = SLOTS * q + i
                        pe.wait_ge(S_h, e + 1)
                        wait(pe, S_hc, e - 1)
                        for s in range(2):
                            last = nc.tensor.transpose(CHT[i % 2][0:FH, s * P:(s + 1) * P], he[:, i % 2, s * FH:(s + 1) * FH], ident[:, :])
                        last.then_inc(S_ht, 1)

                    def down(q, i):
                        e = SLOTS * q + i
                        pe.wait_ge(S_dn[i], 16 * (q + 1))
                        pe.wait_ge(S_hc, e + 1)
                        wait(pe, S_ys, e - 1)
                        for s in range(2):
                            last = nc.tensor.matmul(CO[i % 2][:, :], hT[:, i % 2, s, :], wde[:, i, s, :], start=(s == 0), stop=(s == 1))
                        last.then_inc(S_y, 1)

                    def step(q, i, first=False, last=False):
                        if not last:
                            rows_T(*following(q, i))
                        if not first:
                            h_T(*previous(q, i))
                        gate_up(q, i)
                        if not first:
                            down(*previous(q, i))

                    rows_T(0, 0)
                    steps(pe, step)
                    h_T(E // SLOTS - 1, SLOTS - 1)
                    down(E // SLOTS - 1, SLOTS - 1)

                @block.scalar
                def _(act):
                    def rows_out(q, i):
                        e = SLOTS * q + i
                        act.wait_ge(S_xt, e + 1)
                        wait(act, S_gm, e - 1)
                        nc.scalar.activation(xeT[:, i % 2, :, :], CX[i % 2][:, :].rearrange("p (k q) -> p k q", k=KT), ACT.Copy).then_inc(S_xc, 1)

                    def tanh(q, i):
                        e = SLOTS * q + i
                        act.wait_ge(S_gm, e + 1)
                        wait(act, S_h, e - 1)
                        nc.scalar.activation(te[:, i % 2, :], CG[i % 2][:, 0:FE], ACT.Tanh, scale=0.5).then_inc(S_et, 1)

                    def down(q, i):
                        e = SLOTS * q + i
                        act.wait_ge(S_y, e + 1)
                        act.wait_ge(S_ws, e + 1)
                        if not (isinstance(q, int) and q == 0):
                            act.wait_ge(S_add[i % 2], 16 * (2 * q + i // 2 - 1))
                        nc.scalar.activation(ye[:, i, :], CO[i % 2][:, :], ACT.Copy, scale=wsc[:, i:i + 1]).then_inc(S_ys, 1)

                    def step(q, i, first=False, last=False):
                        if not last:
                            rows_out(*following(q, i))
                        tanh(q, i)
                        if not first:
                            down(*previous(q, i))

                    rows_out(0, 0)
                    steps(act, step)
                    down(E // SLOTS - 1, SLOTS - 1)

                @block.vector
                def _(dve):
                    def gated(q, i):
                        e = SLOTS * q + i
                        dve.wait_ge(S_xe[i], 16 * (q + 1))
                        wait(dve, S_ys, e - SLOTS + 1)
                        if not (isinstance(q, int) and q == 0):
                            dve.wait_ge(S_add[i % 2], 16 * (2 * q + i // 2 - 1))
                        nc.vector.tensor_scalar(wsc[:, i:i + 1], xe[:, i, ds(D + e, 1)], 0.5, None, ALU.mult)
                        nc.vector.tensor_copy(tok[:, i:i + 1], xe[:, i, ROW - 1:ROW]).then_inc(S_ws, 1)
                        dve.wait_ge(S_et, e + 1)
                        nc.vector.scalar_tensor_tensor(out=te[:, i % 2, :], in0=te[:, i % 2, :], scalar=1.0, in1=CG[i % 2][:, 0:FE],
                                                       op0=ALU.add, op1=ALU.mult).then_inc(S_eg, 1)
                        wait(dve, S_ht, e - 1)
                        dve.wait_ge(S_eg, e + 1)
                        nc.vector.tensor_tensor(he[:, i % 2, :], te[:, i % 2, :], CG[i % 2][:, FE:2 * FE], ALU.mult).then_inc(S_h, 1)

                    def copy_T(q, i):
                        e = SLOTS * q + i
                        dve.wait_ge(S_ht, e + 1)
                        wait(dve, S_y, e - 1)
                        nc.vector.tensor_copy(hT[:, i % 2, :, :], CHT[i % 2][0:FH, 0:2 * P].rearrange("p (s q) -> p s q", s=2)).then_inc(S_hc, 1)

                    def step(q, i, first=False, last=False):
                        if not first:
                            copy_T(*previous(q, i))
                        gated(q, i)

                    steps(dve, step)
                    copy_T(E // SLOTS - 1, SLOTS - 1)

                @block.gpsimd
                def _(pool):
                    for e in range(E):
                        pool.wait_ge(S_ys, e + 1)
                        wait(pool, S_add[e % 2], 16 * (e // 2))
                        nc.gpsimd.indirect_dma_start(acc[e % 2][:, :], bass.IndirectOffsetOnAxis(tok[:, e % SLOTS:e % SLOTS + 1], 0),
                                                     ye[:, e % SLOTS, :], None, bounds_check=NROWS - 1, compute_op=ALU.add).then_inc(S_add[e % 2], 16)
                    for s in S_add:
                        pool.wait_ge(s, 16 * E // 2)

        Dd = ExitStack()
        with Dd:
            pa = sb(Dd, "pa", [P, NCH, TT, D])
            pb = sb(Dd, "pb", [P, NCH, TT, D])
            S_ab = [sem(f"sums_in{c}") for c in range(NCH)]
            S_s = sem("summed"); S_out = sem("out_stored")
            with nc.Block() as block:
                @block.sync
                def _(sp):
                    for c in range(NCH):
                        sp.dma_start(pa[:, c], chunk(acc[0], c)).then_inc(S_ab[c], 16)
                        sp.dma_start(pb[:, c], chunk(acc[1], c)).then_inc(S_ab[c], 16)
                    for c in range(NCH):
                        sp.wait_ge(S_s, c + 1)
                        sp.dma_start(chunk(a["out"][0], c), pa[:, c]).then_inc(S_out, 16)
                    sp.wait_ge(S_out, 16 * NCH)

                @block.vector
                def _(dve):
                    for c in range(NCH):
                        dve.wait_ge(S_ab[c], 32)
                        nc.vector.tensor_tensor(pa[:, c], pa[:, c], pb[:, c], ALU.add).then_inc(S_s, 1)


def arrange(i):
    g = {k: np.asarray(v) for k, v in i.items()}
    cols = lambda v: v.reshape(-1, P).T
    m = {
        "x": g["L0_attn_x"],
        "wxpT": g["L0_attn_W_xproj"].T, "wdtT": g["L0_attn_W_dt"].T, "A_log": g["L0_attn_A_log"],
        "vec": np.concatenate([cols(g["L0_attn_b_dt"]), cols(g["L0_attn_D_param"]), cols(g["L0_ffn_SU_ug"]),
                               cols(g["L0_ffn_SU_dp"]), cols(g["L0_ffn_Wscale_ug"][F0:]), cols(g["L0_ffn_Wscale_ug"][:F0])], 1),
        "ws_dp": g["L0_ffn_Wscale_dp"],
        "wuT": g["L0_ffn_W_up"].T, "wgT": g["L0_ffn_W_gate"].T, "wdT": g["L0_ffn_W_down"].T,
        "winx": g["L1_attn_W_in"][:I1], "winzT": g["L1_attn_W_in"][I1:].T,
        "convT": g["L1_attn_conv_w"].T, "d1": cols(g["L1_attn_D"]), "woT": g["L1_attn_W_out"].T,
        "gateT": g["L1_ffn_gate_w"].T, "wg": g["L1_ffn_wg"], "wu": g["L1_ffn_wu"], "wd": g["L1_ffn_wd"],
    }
    h = hadamard(P).astype(np.float32)
    sel = np.zeros((P, 2 * NS), np.float32)
    for n in range(2 * NS):
        sel[R + n, n] = sel[R + 2 * NS + n, n] = 1
    m["ident"] = np.eye(P, dtype=np.float32)
    m["had"] = np.concatenate([h, -h], 1)
    m["sel"] = sel
    m["before"] = np.triu(np.ones((P, P), np.float32), 1)
    m["first_slot"] = np.broadcast_to((np.arange(E) * P + 1).astype(np.float32), (P, E))
    m["empty"] = np.concatenate([np.zeros((P, D + E), np.float32), (T + np.arange(P, dtype=np.float32)).reshape(P, 1)], 1)
    m["number"] = np.arange(P, dtype=np.float32).reshape(P, 1)
    return {k: np.ascontiguousarray(v) for k, v in m.items()}


def kernel(**inputs):
    import concourse.bacc as bacc
    from concourse import mybir
    from concourse.bass_utils import run_bass_kernel_spmd

    nc = bacc.Bacc("TRN2", target_bir_lowering=False, num_devices=1, dynamic_dma_scratch_size=8192)
    arrays = arrange(inputs)
    a = {k: nc.dram_tensor(k + "_in", v.shape, mybir.dt.from_np(v.dtype), kind="ExternalInput").ap() for k, v in arrays.items()}
    for name, shape in (("x2", (T, D)), ("acc0", (NROWS, D)), ("acc1", (NROWS, D)), ("slots", (E * P, ROW)),
                        ("w_up", (M0, P, KT, 2, P)), ("w_down", (M0, P, 2, D))):
        a[name] = nc.dram_tensor(name, shape, mybir.dt.float32, kind="Internal").ap()
    a["out"] = nc.dram_tensor("out", (1, T, D), mybir.dt.float32, kind="ExternalOutput").ap()
    build(nc, a)
    r = run_bass_kernel_spmd(nc, [{k + "_in": v for k, v in arrays.items()}], core_ids=[0])
    return r.results[0]["out"]
```
